# Optimizing a Trainium2 kernel written in Bass

```python
import numpy as np
import jax
import jax.numpy as jnp

def _softmax(x, axis=-1):
    return jax.nn.softmax(x, axis=axis)

def _gelu(x):
    return jax.nn.gelu(x, approximate=True)

def _silu(x):
    return jax.nn.silu(x)

def _sigmoid(x):
    return jax.nn.sigmoid(x)

def _layernorm(x, axis=-1, eps=1e-05):
    m = jnp.mean(x, axis=axis, keepdims=True)
    v = jnp.var(x, axis=axis, keepdims=True)
    return (x - m) / jnp.sqrt(v + eps)

def _scatter_add(tgt, idx, src, axis=0):
    return tgt.at[idx].add(src)

def _segment_sum(src, seg, n):
    return jax.ops.segment_sum(src, seg, n)
kernel_name = 'mk_adj_ffn_d1_adj_r2_36823b'

def setup_inputs(seed: int=0):
    np.random.seed(seed)
    _w = jnp.asarray

    def _rec_inputs():
        import jax
        import jax.numpy as jnp
        _gk = jax.random.key(seed)
        x = -0.0002928 + 1 * jax.random.normal(jax.random.fold_in(_gk, 1), (128, 64, 128), jnp.float32)
        _a = jax.random.bernoulli(jax.random.fold_in(_gk, 2), 0.125, (64, 64))
        _a = jnp.logical_or(_a, jnp.swapaxes(_a, -1, -2))
        _a = jnp.logical_or(_a, jnp.eye(64, dtype=bool))
        adj = _a.astype(jnp.int32)
        return (x, adj)
    x, adj = _rec_inputs()

    def _L0_gnn_setup():
        import jax, jax.numpy as jnp
        import numpy as np
        ALPHA = 0.2
        NEG_INF = -1000000000000.0
        key = jax.random.key(seed)
        k1, k2, k3, k4, k5 = jax.random.split(key, 5)
        B, N, C_in, C_out = (8, 1024, 128, 128)
        inp = jax.random.normal(k1, (B, N, C_in), dtype=jnp.float32)
        adj = jax.random.randint(k2, (N, N), 0, 2, dtype=jnp.int32)
        limit = 1.414 * np.sqrt(6.0 / (C_in + C_out))
        W1 = jax.random.uniform(k3, (C_in, C_out), jnp.float32, -limit, limit)
        W2 = jax.random.uniform(k4, (C_in, C_out), jnp.float32, -limit, limit)
        W3 = jax.random.uniform(k5, (C_in, C_out), jnp.float32, -limit, limit)
        return {'inp': inp, 'adj': adj, 'W1': W1, 'W2': W2, 'W3': W3}
    _L0_gnn_all = _L0_gnn_setup()
    _L0_gnn_in = {k: v for k, v in _L0_gnn_all.items() if k in ('W1', 'W2', 'W3')}
    del _L0_gnn_all

    def _L0_ffn_setup():
        import jax, jax.numpy as jnp
        import numpy as np
        N_EXPERTS = 8
        TOP_K = 2
        key = jax.random.key(seed)
        ks = jax.random.split(key, 5)
        B, T, C, E, H = (8, 1024, 128, 8, 341)
        scale = 1.0 / np.sqrt(C)
        return {'x': jax.random.normal(ks[0], (B, T, C), dtype=jnp.float32), 'router_w': jax.random.normal(ks[1], (E, C), dtype=jnp.float32) * scale, 'w1': jax.random.normal(ks[2], (E, H, C), dtype=jnp.float32) * scale, 'w2': jax.random.normal(ks[3], (E, C, H), dtype=jnp.float32) * (1.0 / np.sqrt(H)), 'w3': jax.random.normal(ks[4], (E, H, C), dtype=jnp.float32) * scale}
    _L0_ffn_all = _L0_ffn_setup()
    _L0_ffn_in = {k: v for k, v in _L0_ffn_all.items() if k in ('router_w', 'w1', 'w2', 'w3')}
    del _L0_ffn_all
    return {'x': x, 'adj': adj, 'L0_gnn_W1': _L0_gnn_in['W1'], 'L0_gnn_W2': _L0_gnn_in['W2'], 'L0_gnn_W3': _L0_gnn_in['W3'], 'L0_ffn_router_w': _L0_ffn_in['router_w'], 'L0_ffn_w1': _L0_ffn_in['w1'], 'L0_ffn_w2': _L0_ffn_in['w2'], 'L0_ffn_w3': _L0_ffn_in['w3']}

def reference(x, adj, L0_gnn_W1, L0_gnn_W2, L0_gnn_W3, L0_ffn_router_w, L0_ffn_w1, L0_ffn_w2, L0_ffn_w3):
    import jax
    import jax.numpy as jnp

    def _L0_gnn_ref(inp, adj, W1, W2, W3):
        import jax, jax.numpy as jnp
        import numpy as np
        ALPHA = 0.2
        NEG_INF = -1000000000000.0
        h1 = jnp.einsum('bnc,cd->bnd', inp, W1)
        h2 = jnp.einsum('bnc,cd->bnd', inp, W2)
        h3 = jnp.einsum('bnc,cd->bnd', inp, W3)
        e = jnp.einsum('bnd,bmd->bnm', h1, h2)
        e = jax.nn.leaky_relu(e, ALPHA)
        e = jnp.where(adj[None, :, :] > 0, e, NEG_INF)
        attention = jax.nn.softmax(e, axis=-1)
        h_prime = jnp.einsum('bnm,bmd->bnd', attention, h3)
        return jax.nn.relu(h_prime)

    def _L0_ffn_ref(x, router_w, w1, w2, w3):
        import jax, jax.numpy as jnp
        import numpy as np
        N_EXPERTS = 8
        TOP_K = 2
        B, T, C = x.shape
        flat = x.reshape(-1, C)
        logits = flat @ router_w.T
        probs = jax.nn.softmax(logits, axis=-1)
        topk_probs, topk_idx = jax.lax.top_k(probs, TOP_K)
        topk_probs = topk_probs / (jnp.sum(topk_probs, axis=-1, keepdims=True) + 1e-09)
        onehot = jax.nn.one_hot(topk_idx, N_EXPERTS, dtype=flat.dtype)
        gates = jnp.einsum('nk,nke->ne', topk_probs, onehot)
        h1 = jnp.einsum('nc,ehc->neh', flat, w1)
        h3 = jnp.einsum('nc,ehc->neh', flat, w3)
        h = jax.nn.silu(h1) * h3
        y = jnp.einsum('neh,ech->nec', h, w2)
        out = jnp.einsum('ne,nec->nc', gates, y)
        return out.reshape(B, T, C)
    x = x + _L0_gnn_ref(_layernorm(x, axis=-1), adj, L0_gnn_W1, L0_gnn_W2, L0_gnn_W3)
    x = x + _L0_ffn_ref(_layernorm(x, axis=-1), L0_ffn_router_w, L0_ffn_w1, L0_ffn_w2, L0_ffn_w3)
    return x

_drawn_inputs = setup_inputs


def setup_inputs(seed=0):
    import zlib

    import numpy as np

    out = dict(_drawn_inputs(seed))
    spreads = {}
    factors = {}
    for name, (base, spread) in spreads.items():
        noise = np.random.default_rng([zlib.crc32(name.encode()), seed]).standard_normal(out[name].shape)
        drawn = base * np.exp(spread * noise) if base else spread * noise
        out[name] = jnp.asarray(drawn.astype(out[name].dtype))
    for name, factor in factors.items():
        out[name] = (out[name] * factor).astype(out[name].dtype)
    return out
```

```python
from contextlib import ExitStack

import concourse.bass as bass
from concourse import mybir


BATCH, N, C = 128, 64, 128
E, H = 8, 341
P = 128
T = BATCH * N
BT = 512
NB = T // BT
TI = BT // P
FULL = H // P
REST = H - FULL * P
PURE = E * FULL
MIXED = -(-E * REST // P)
CH = PURE + MIXED
LAG = 3
ALPHA, NEG, EPS, TOP_EPS = 0.2, 1e12, 1e-5, 1e-9

SEGMENTS = []
for _k in range(MIXED):
    _p = 0
    while _p < P:
        _e = min((_k * P + _p) // REST, E - 1)
        _end = P if _e == E - 1 else min(P, (_e + 1) * REST - _k * P)
        SEGMENTS.append((_k, _p, _end, _e))
        _p = _end
GATE_DMAS = 1 + len(SEGMENTS)

FIRST_HALF = 9


def bass_gnn_moe_kernel(nc, x, adj, gnn_w1T, gnn_w2T, gnn_w3, routerT, w1T, w3T, w2, outT):
    fp32, fp32r, i32 = mybir.dt.float32, mybir.dt.float32r, mybir.dt.int32
    ALU, ACT, X = mybir.AluOpType, mybir.ActivationFunctionType, mybir.AxisListType.X
    PE, DVE, SCA, POOL, SP = nc.tensor, nc.vector, nc.scalar, nc.gpsimd, nc.sync

    x_blocks = x.rearrange("(b t p) c -> p b t c", t=TI, p=P)
    gate_rows = [nc.dram_tensor(f"gate_rows{i}", (E, BT), fp32).ap() for i in range(2)]

    with ExitStack() as ctx:
        def sb(name, shape, dt=fp32):
            return ctx.enter_context(nc.sbuf_tensor(name, shape, dt))

        def pair(name, shape, dt=fp32, n=2):
            return [sb(f"{name}{i}", shape, dt) for i in range(n)]

        def bank(name):
            return ctx.enter_context(nc.psum_tensor(name, [P, BT], fp32))

        def sem(name):
            return ctx.enter_context(nc.semaphore(name))

        ident = sb("ident", [P, P])
        adj_sb = sb("adj_sb", [P, N], i32)
        mask = sb("mask", [P, TI, N])
        no_edge = sb("no_edge", [P, TI, N])
        earlier = sb("earlier", [P, TI, E, E])
        minus_half, eps = sb("minus_half", [P, TI]), sb("eps", [P, TI])
        g1T, g2T, g3 = sb("g1T", [P, C]), sb("g2T", [P, C]), sb("g3", [P, C])
        scores_w = sb("scores_w", [P, C])
        rw = sb("rw", [P, P])
        rw_hi, rw_lo = sb("rw_hi", [P, P], fp32r), sb("rw_lo", [P, P], fp32r)
        w1_hi, w1_lo = sb("w1_hi", [P, CH, P], fp32r), sb("w1_lo", [P, CH, P], fp32r)
        w3_hi, w3_lo = sb("w3_hi", [P, CH, P], fp32r), sb("w3_lo", [P, CH, P], fp32r)
        w2_hi, w2_lo = sb("w2_hi", [P, CH, P], fp32r), sb("w2_lo", [P, CH, P], fp32r)
        gate = pair("gate", [P, E + MIXED, BT])
        w1_in = gate[1][:, 0:6, :].rearrange("p a b -> p (a b)")[:, 0:CH * P].rearrange("p (c k) -> p c k", k=P)
        w3_in = gate[1][:, 6:12, :].rearrange("p a b -> p (a b)")[:, 0:CH * P].rearrange("p (c k) -> p c k", k=P)
        w2_in = gate[0][:, 0:6, :].rearrange("p a b -> p (a b)")[:, 0:CH * P].rearrange("p (c k) -> p c k", k=P)

        x_in = pair("x_in", [P, TI, C])
        stats = sb("stats", [P, TI, 6])
        mean, apart, squares = sb("mean", [P, TI]), sb("apart", [P, TI]), sb("squares", [P, TI])
        var_eps = sb("var_eps", [P, TI])
        rstd = sb("rstd", [P, TI])
        xn = sb("xn", [P, TI, C])
        xnT = sb("xnT", [P, BT])
        qT = sb("qT", [P, BT])
        v = sb("v", [P, TI, C])
        small_e = sb("small_e", [P, TI, N])
        scores = sb("scores", [P, TI, N])
        row_max = sb("row_max", [P, TI])
        probs = sb("probs", [P, TI, P])
        row_sum = sb("row_sum", [P, TI])
        row_scale = sb("row_scale", [P, TI])
        probsT = sb("probsT", [P, TI, P])
        att = sb("att", [P, TI, C])
        x2 = pair("x2", [P, TI, C])
        xT_hi, xT_lo = pair("xT_hi", [P, BT], fp32r), pair("xT_lo", [P, BT], fp32r)
        logitsT = sb("logitsT", [P, BT])
        logits = sb("logits", [P, TI, E])
        top = sb("top", [P, TI])
        shifted = sb("shifted", [P, TI, E])
        expo = sb("expo", [P, TI, E])
        total = sb("total", [P, TI])
        prob = sb("prob", [P, TI, E])
        above = sb("above", [P, TI, E, E])
        tied = sb("tied", [P, TI, E, E])
        rank = sb("rank", [P, TI, E])
        gates = sb("gates", [P, TI, E])
        gatesT = sb("gatesT", [TI * E, P])
        act = pair("act", [P, BT])
        gated = pair("gated", [P, BT])
        hid = pair("hid", [P, BT])
        hid_hi, hid_lo = pair("hid_hi", [P, BT], fp32r, 4), pair("hid_lo", [P, BT], fp32r, 4)
        y_out = sb("y_out", [P, BT])

        h1_ps, h3_ps = [bank("h1_ps0"), bank("h1_ps1")], [bank("h3_ps0"), bank("h3_ps1")]
        y_ps = bank("y_ps")
        A, B = bank("att_ps0"), bank("att_ps1")

        gnn_in, adj_in, x_arrived = sem("gnn_in"), sem("adj_in"), sem("x_arrived")
        w1_arrived, w3_arrived, w2_arrived = sem("w1_arrived"), sem("w3_arrived"), sem("w2_arrived")
        pool_step, dve_step, sum_step = sem("pool_step"), sem("dve_step"), sem("sum_step")
        ident_set, consts_set, masks_set = sem("ident_set"), sem("consts_set"), sem("masks_set")
        wprod_ps, wprod_set = sem("wprod_ps"), sem("wprod_set")
        hi_split, lo_split_dve, lo_split_pool = sem("hi_split"), sem("lo_split_dve"), sem("lo_split_pool")
        moments1, rstd1, xn_set, xT_ps, xT_set = (sem(n) for n in ("moments1", "rstd1", "xn_set", "xT_ps", "xT_set"))
        q_ps, q_set, v_ps, v_set, e_ps = (sem(n) for n in ("q_ps", "q_set", "v_ps", "v_set", "e_ps"))
        small_set, leaky_set, masked_set, shifted_set = (sem(n) for n in ("small_set", "leaky_set", "masked_set", "shifted_set"))
        probs_set, scale_set, pT_ps, pT_set, pv_ps = (sem(n) for n in ("probs_set", "scale_set", "pT_ps", "pT_set", "pv_ps"))
        att_set, x2_set, moments2, rstd2, xn2_set = (sem(n) for n in ("att_set", "x2_set", "moments2", "rstd2", "xn2_set"))
        x2T_ps, xhi_set, xlo_set, lgT_ps, lgT_set = (sem(n) for n in ("x2T_ps", "xhi_set", "xlo_set", "lgT_ps", "lgT_set"))
        lg_ps, lg_shifted, lg_exp, gates_set, gT_ps = (sem(n) for n in ("lg_ps", "lg_shifted", "lg_exp", "gates_set", "gT_ps"))
        gT_set, rows_written, gate_loaded, lg_set = (sem(n) for n in ("gT_set", "rows_written", "gate_loaded", "lg_set"))
        h1_done, h3_done, act_set, gated_set = (sem(n) for n in ("h1_done", "h3_done", "act_set", "gated_set"))
        hid_set, hhi_set, hlo_set, w2_done = (sem(n) for n in ("hid_set", "hhi_set", "hlo_set", "w2_done"))
        y_set, out_stored = sem("y_set"), sem("out_stored")

        block = ctx.enter_context(nc.Block())

        def wait(eng, s, count):
            if not isinstance(count, int) or count > 0:
                eng.wait_ge(s, count)

        def over_blocks(eng, start, body):
            start()
            body(0, 0, True, True)
            with eng.Fori(0, (NB - 4) // 2) as i:
                body(i * 2 + 1, 1, True, True)
                body(i * 2 + 2, 0, True, True)
            body(NB - 3, 1, True, True)
            body(NB - 2, 0, True, False)
            body(NB - 1, 1, False, False)

        @block.sync
        def _(sp):
            def load_x(n, par):
                wait(sp, xn_set, n)
                sp.dma_start(x_in[par][:], x_blocks[:, bass.ds(n, 1)].rearrange("p b t c -> p (b t) c")
                             if not isinstance(n, int) else x_blocks[:, n]).then_inc(x_arrived, 16)

            def load_gates(n, par):
                wait(sp, gated_set, (n - 1) * CH)
                sp.wait_ge(gT_set, n + 1)
                sp.dma_start(gate_rows[par].rearrange("e (t p) -> t e p", t=TI), gatesT[:]).then_inc(rows_written, 16)
                sp.wait_ge(rows_written, n * 16 + 16)
                sp.dma_start(gate[par][:, 0:E, :].rearrange("p e t -> p (e t)"),
                             gate_rows[par].rearrange("e t -> (e t)").partition_broadcast(P)).then_inc(gate_loaded, 16)
                for k, p0, p1, e in SEGMENTS:
                    sp.dma_start(gate[par][p0:p1, E + k, :],
                                 gate_rows[par][e].partition_broadcast(p1 - p0)).then_inc(gate_loaded, 16)

            def store_out(n):
                sp.wait_ge(y_set, n + 1)
                sp.dma_start(outT[:, bass.ds(n * BT, BT)], y_out[:]).then_inc(out_stored, 16)

            def start():
                load_x(0, 0)
                sp.dma_start(g1T[:], gnn_w1T).then_inc(gnn_in, 16)
                sp.dma_start(g2T[:], gnn_w2T).then_inc(gnn_in, 16)
                sp.dma_start(g3[:], gnn_w3).then_inc(gnn_in, 16)
                sp.dma_start(rw[:], routerT).then_inc(gnn_in, 16)
                sp.dma_start(adj_sb[0:N, :], adj).then_inc(adj_in, 16)
                sp.dma_start(adj_sb[N:P, :], adj).then_inc(adj_in, 16)
                sp.dma_start(w1_in, w1T.rearrange("c (k h) -> c k h", h=P)).then_inc(w1_arrived, 16)
                sp.dma_start(w3_in, w3T.rearrange("c (k h) -> c k h", h=P)).then_inc(w3_arrived, 16)
                sp.dma_start(w2_in, w2.rearrange("(k h) c -> h k c", h=P)).then_inc(w2_arrived, 16)
                load_x(1, 1)
                sp.wait_ge(hi_split, 4)
                sp.wait_ge(lo_split_dve, 1)
                sp.wait_ge(lo_split_pool, 2)
                load_gates(0, 0)

            def body(b, par, second, first):
                if first:
                    load_x(b + 2, par)
                if not isinstance(b, int) or b > 0:
                    store_out(b - 1)
                if second:
                    load_gates(b + 1, 1 - par)

            over_blocks(sp, start, body)
            store_out(NB - 1)
            sp.wait_ge(out_stored, NB * 16)

        @block.tensor
        def _(pe):
            def split_product(out, hi_w, lo_w, hi_x, lo_x, start=True, stop=True):
                PE.matmul(out, hi_w, hi_x, start=start, stop=False, skip_group_check=True)
                PE.matmul(out, hi_w, lo_x, start=False, stop=False, skip_group_check=True)
                return PE.matmul(out, lo_w, hi_x, start=False, stop=stop, skip_group_check=True)

            def first_half(n, par, c):
                if c == 2:
                    pe.wait_ge(xn_set, n + 1)
                    wait(pe, lg_set, n)
                    for t in range(TI):
                        last = PE.transpose(A[:, t * P:(t + 1) * P], xn[:, t, :], ident[:])
                    last.then_inc(xT_ps, 1)
                if c == 4:
                    pe.wait_ge(xT_set, n + 1)
                    wait(pe, gT_set, n)
                    PE.matmul(B[:], scores_w[:], xnT[:], start=True, stop=True).then_inc(q_ps, 1)
                    for t in range(TI):
                        last = PE.matmul(A[:, t * P:(t + 1) * P], xnT[:, t * P:(t + 1) * P], g3[:],
                                         start=True, stop=True, skip_group_check=True)
                    last.then_inc(v_ps, 1)
                if c == 6:
                    pe.wait_ge(q_set, n + 1)
                    for t in range(TI):
                        for g in range(2):
                            at = t * P + g * N
                            last = PE.matmul(B[g * N:(g + 1) * N, t * N:(t + 1) * N], qT[:, at:at + N],
                                             xnT[:, at:at + N], start=True, stop=True, skip_group_check=True)
                    last.then_inc(e_ps, 1)
                if c == 10:
                    pe.wait_ge(probs_set, n + 1)
                    pe.wait_ge(v_set, n + 1)
                    for t in range(TI):
                        last = PE.transpose(A[:, t * P:(t + 1) * P], probs[:, t, :], ident[:])
                    last.then_inc(pT_ps, 1)
                if c == 12:
                    pe.wait_ge(pT_set, n + 1)
                    for t in range(TI):
                        last = PE.matmul(B[:, t * P:(t + 1) * P], probsT[:, t, :], v[:, t, :],
                                         start=True, stop=True, skip_group_check=True)
                    last.then_inc(pv_ps, 1)

            def second_half(n, par, c):
                if c == 2:
                    pe.wait_ge(xn2_set, n + 1)
                    for t in range(TI):
                        last = PE.transpose(A[:, t * P:(t + 1) * P], xn[:, t, :], ident[:])
                    last.then_inc(x2T_ps, 1)
                if c == 4:
                    pe.wait_ge(xlo_set, n + 1)
                    pe.wait_ge(att_set, n + 1)
                    split_product(B[:], rw_hi[:], rw_lo[:], xT_hi[par][:], xT_lo[par][:]).then_inc(lgT_ps, 1)
                if c == 5:
                    pe.wait_ge(lgT_set, n + 1)
                    for t in range(TI):
                        last = PE.transpose(A[:, t * P:(t + 1) * P], logitsT[:, t * P:(t + 1) * P], ident[:])
                    last.then_inc(lg_ps, 1)
                if c == 8:
                    pe.wait_ge(gates_set, n + 1)
                    PE.transpose(B[0:TI * E, 0:P], gates[:].rearrange("p t e -> p (t e)"),
                                 ident[:]).then_inc(gT_ps, 1)

            def start():
                pe.wait_ge(gnn_in, 64)
                PE.matmul(B[:, 0:C], g1T[:], g2T[:], start=True, stop=True).then_inc(wprod_ps, 1)
                pe.wait_ge(ident_set, 1)
                pe.wait_ge(wprod_set, 1)
                for c in range(CH):
                    first_half(0, 0, c)
                for c in range(CH):
                    second_half(0, 0, c)
                for c in range(CH):
                    first_half(1, 1, c)

            def body(b, par, second, first):
                pe.wait_ge(xlo_set, b + 1)
                for c in range(CH):
                    g, i = b * CH + c, (par * CH + c)
                    if isinstance(b, int) and b == 0 and c == 0:
                        pe.wait_ge(lo_split_dve, 1)
                        pe.wait_ge(lo_split_pool, 1)
                    wait(pe, act_set, g - 1)
                    split_product(h1_ps[i % 2][:], w1_hi[:, c, :], w1_lo[:, c, :],
                                  xT_hi[par][:], xT_lo[par][:]).then_inc(h1_done, 1)
                    wait(pe, gated_set, g - 1)
                    split_product(h3_ps[i % 2][:], w3_hi[:, c, :], w3_lo[:, c, :],
                                  xT_hi[par][:], xT_lo[par][:]).then_inc(h3_done, 1)
                    if c >= LAG:
                        pe.wait_ge(hlo_set, g - LAG + 1)
                        if c == LAG:
                            if isinstance(b, int) and b == 0:
                                pe.wait_ge(lo_split_pool, 2)
                            wait(pe, y_set, b)
                        split_product(y_ps[:], w2_hi[:, c - LAG, :], w2_lo[:, c - LAG, :],
                                      hid_hi[(i - LAG) % 4][:], hid_lo[(i - LAG) % 4][:],
                                      start=(c == LAG), stop=False).then_inc(w2_done, 1)
                        if c == LAG:
                            for t in range(TI):
                                PE.matmul(y_ps[:, t * P:(t + 1) * P], x2[par][:, t, :], ident[:],
                                          start=False, stop=False, skip_group_check=True)
                    elif not isinstance(b, int) or b > 0:
                        tail_product(b, par, c)
                    if second:
                        second_half(b + 1, 1 - par, c)
                    if first and c >= FIRST_HALF:
                        first_half(b + 2, par, c - FIRST_HALF)

            def tail_product(b, par, c):
                g, i = b * CH + c - LAG, (par * CH + c - LAG) % 4
                k = CH - LAG + c
                pe.wait_ge(hlo_set, g + 1)
                split_product(y_ps[:], w2_hi[:, k, :], w2_lo[:, k, :], hid_hi[i][:], hid_lo[i][:],
                              start=False, stop=(k == CH - 1)).then_inc(w2_done, 1)

            over_blocks(pe, start, body)
            for c in range(LAG):
                tail_product(NB, 0, c)

        @block.scalar
        def _(sc):
            def first_half(n, par, c):
                if c == 3:
                    sc.wait_ge(xT_ps, n + 1)
                    SCA.activation(xnT[:], A[:], ACT.Copy).then_inc(xT_set, 1)
                if c == 5:
                    sc.wait_ge(v_ps, n + 1)
                    SCA.activation(v[:].rearrange("p t c -> p (t c)"), A[:], ACT.Copy).then_inc(v_set, 1)
                if c == 7:
                    sc.wait_ge(e_ps, n + 1)
                    SCA.activation(small_e[:].rearrange("p t c -> p (t c)"), B[:, 0:TI * N], ACT.Copy,
                                   scale=ALPHA).then_inc(small_set, 1)
                if c == 9:
                    sc.wait_ge(shifted_set, n + 1)
                    for g in range(2):
                        at = slice(g * N, (g + 1) * N)
                        last = SCA.activation(probs[at, :, at], scores[at, :, :], ACT.Exp)
                    last.then_inc(probs_set, 1)
                if c == 12:
                    sc.wait_ge(pv_ps, n + 1)
                    sc.wait_ge(scale_set, n + 1)
                    for t in range(TI):
                        last = SCA.activation(att[:, t, :], B[:, t * P:(t + 1) * P], ACT.Relu,
                                              scale=row_scale[:, t:t + 1])
                    last.then_inc(att_set, 1)

            def second_half(n, par, c):
                if c == 3:
                    sc.wait_ge(x2T_ps, n + 1)
                    SCA.activation(xT_hi[par][:], A[:], ACT.Copy).then_inc(xhi_set, 1)
                if c == 6:
                    sc.wait_ge(lg_shifted, n + 1)
                    SCA.activation(expo[:].rearrange("p t e -> p (t e)"),
                                   shifted[:].rearrange("p t e -> p (t e)"), ACT.Exp).then_inc(lg_exp, 1)

            def coarse(g, i):
                sc.wait_ge(hid_set, g + 1)
                wait(sc, w2_done, g - 3)
                SCA.activation(hid_hi[i % 4][:], hid[i % 2][:], ACT.Copy).then_inc(hhi_set, 1)

            def start():
                sc.wait_ge(wprod_ps, 1)
                SCA.activation(scores_w[:], B[:, 0:C], ACT.Copy).then_inc(wprod_set, 1)
                SCA.activation(rw_hi[:], rw[:], ACT.Copy).then_inc(hi_split, 1)
                sc.wait_ge(w1_arrived, 16)
                SCA.activation(w1_hi[:], w1_in, ACT.Copy).then_inc(hi_split, 1)
                for c in range(CH):
                    first_half(0, 0, c)
                    if c == 8:
                        sc.wait_ge(w3_arrived, 16)
                        SCA.activation(w3_hi[:], w3_in, ACT.Copy).then_inc(hi_split, 1)
                    if c == 10:
                        sc.wait_ge(w2_arrived, 16)
                        SCA.activation(w2_hi[:], w2_in, ACT.Copy).then_inc(hi_split, 1)
                for c in range(CH):
                    second_half(0, 0, c)
                for c in range(CH):
                    first_half(1, 1, c)

            def body(b, par, second, first):
                for c in range(CH):
                    g, i = b * CH + c, par * CH + c
                    sc.wait_ge(h1_done, g + 1)
                    wait(sc, hid_set, g - 1)
                    SCA.activation(act[i % 2][:], h1_ps[i % 2][:], ACT.Silu).then_inc(act_set, 1)
                    if not isinstance(g, int) or g > 0:
                        coarse(g - 1, i - 1)
                    if c == LAG and (not isinstance(b, int) or b > 0):
                        result(b - 1)
                    if second:
                        second_half(b + 1, 1 - par, c)
                    if first and c >= FIRST_HALF:
                        first_half(b + 2, par, c - FIRST_HALF)

            def result(n):
                sc.wait_ge(w2_done, n * CH + CH)
                wait(sc, out_stored, n * 16)
                SCA.activation(y_out[:], y_ps[:], ACT.Copy).then_inc(y_set, 1)

            over_blocks(sc, start, body)
            coarse(NB * CH - 1, 2 * CH - 1)
            result(NB - 1)

        @block.vector
        def _(dve):
            done = [0]
            STEPS1, STEPS2 = 5, 16
            STEPS = STEPS1 + STEPS2

            def step(instruction, base):
                done[0] += 1
                instruction.then_inc(dve_step, 1)
                dve.wait_ge(dve_step, base + done[0])

            def moments(source, base, signal):
                for t in range(TI):
                    last = DVE.bn_stats(stats[:, t, :], source[:, t, :])
                step(last, base)
                DVE.tensor_tensor(mean[:], stats[:, :, 1], stats[:, :, 4], ALU.add)
                DVE.tensor_tensor(apart[:], stats[:, :, 1], stats[:, :, 4], ALU.subtract)
                step(DVE.tensor_tensor(squares[:], stats[:, :, 2], stats[:, :, 5], ALU.add), base)
                DVE.tensor_scalar(mean[:], mean[:], 0.5, None, ALU.mult)
                step(DVE.tensor_tensor(apart[:], apart[:], apart[:], ALU.mult), base)
                step(DVE.scalar_tensor_tensor(squares[:], apart[:], C / 4, squares[:], ALU.mult, ALU.add), base)
                DVE.tensor_scalar(var_eps[:], squares[:], 1 / C, EPS, ALU.mult, ALU.add).then_inc(signal, 1)

            def first_half(n, par, c):
                base = n * STEPS + 2
                if c == 0:
                    done[0] = 0
                    dve.wait_ge(x_arrived, n * 16 + 16)
                    wait(dve, rstd2, n)
                    moments(x_in[par], base, moments1)
                if c == 1:
                    dve.wait_ge(rstd1, n + 1)
                    wait(dve, x2T_ps, n)
                    for t in range(TI):
                        last = DVE.tensor_scalar(xn[:, t, :], x_in[par][:, t, :], mean[:, t:t + 1],
                                                 rstd[:, t:t + 1], ALU.subtract, ALU.mult)
                    last.then_inc(xn_set, 1)
                if c == 5:
                    dve.wait_ge(q_ps, n + 1)
                    DVE.tensor_copy(qT[:], B[:]).then_inc(q_set, 1)
                if c == 7:
                    dve.wait_ge(small_set, n + 1)
                    DVE.tensor_tensor(scores[:].rearrange("p t m -> p (t m)"), B[:, 0:TI * N],
                                      small_e[:].rearrange("p t m -> p (t m)"), ALU.max).then_inc(leaky_set, 1)
                if c == 8:
                    dve.wait_ge(masked_set, n + 1)
                    step(DVE.reduce_max(row_max[:], scores[:], axis=X), base)
                    DVE.tensor_tensor(scores[:], scores[:], row_max[:].unsqueeze(2).broadcast_to([P, TI, N]),
                                      ALU.subtract).then_inc(shifted_set, 1)
                if c == 10:
                    dve.wait_ge(probs_set, n + 1)
                    step2(DVE.reduce_sum(row_sum[:], probs[:], axis=X), n)
                    DVE.reciprocal(row_scale[:], row_sum[:]).then_inc(scale_set, 1)
                if c == 11:
                    dve.wait_ge(pT_ps, n + 1)
                    DVE.tensor_copy(probsT[:].rearrange("p t m -> p (t m)"), A[:]).then_inc(pT_set, 1)

            def step2(instruction, n):
                instruction.then_inc(sum_step, 1)
                dve.wait_ge(sum_step, n + 1)

            def second_half(n, par, c):
                base = n * STEPS + 2 + STEPS1
                if c == 0:
                    done[0] = 0
                    dve.wait_ge(x2_set, n + 1)
                    moments(x2[par], base, moments2)
                if c == 1:
                    dve.wait_ge(rstd2, n + 1)
                    for t in range(TI):
                        last = DVE.tensor_scalar(xn[:, t, :], x2[par][:, t, :], mean[:, t:t + 1],
                                                 rstd[:, t:t + 1], ALU.subtract, ALU.mult)
                    last.then_inc(xn2_set, 1)
                if c == 3:
                    dve.wait_ge(xhi_set, n + 1)
                    DVE.tensor_tensor(xT_lo[par][:], A[:], xT_hi[par][:].bitcast(fp32),
                                      ALU.subtract).then_inc(xlo_set, 1)
                if c == 5:
                    dve.wait_ge(lgT_ps, n + 1)
                    DVE.tensor_copy(logitsT[:], B[:]).then_inc(lgT_set, 1)
                if c == 6:
                    dve.wait_ge(lg_ps, n + 1)
                    ins = DVE.tensor_copy(logits[:], A[:].rearrange("p (t e) -> p t e", t=TI)[:, :, 0:E])
                    ins.then_inc(lg_set, 1)
                    dve.wait_ge(lg_set, n + 1)
                    step(DVE.reduce_max(top[:], logits[:], axis=X), base)
                    DVE.tensor_tensor(shifted[:], logits[:], top[:].unsqueeze(2).broadcast_to([P, TI, E]),
                                      ALU.subtract).then_inc(lg_shifted, 1)
                if c == 7:
                    dve.wait_ge(lg_exp, n + 1)
                    per_token = lambda a: a[:].unsqueeze(2).broadcast_to([P, TI, E])
                    this = prob[:].unsqueeze(3).broadcast_to([P, TI, E, E])
                    other = prob[:].unsqueeze(2).broadcast_to([P, TI, E, E])
                    step(DVE.reduce_sum(total[:], expo[:], axis=X), base)
                    step(DVE.reciprocal(top[:], total[:]), base)
                    step(DVE.tensor_tensor(prob[:], expo[:], per_token(top), ALU.mult), base)
                    DVE.tensor_tensor(above[:], other, this, ALU.is_gt)
                    step(DVE.tensor_tensor(tied[:], other, this, ALU.is_equal), base)
                    step(DVE.tensor_tensor(tied[:], tied[:], earlier[:], ALU.mult), base)
                    step(DVE.tensor_tensor(above[:], above[:], tied[:], ALU.add), base)
                    step(DVE.reduce_sum(rank[:], above[:], axis=X), base)
                    step(DVE.scalar_tensor_tensor(gates[:], rank[:], 1.5, prob[:], ALU.is_lt, ALU.mult), base)
                    step(DVE.reduce_sum(total[:], gates[:], axis=X), base)
                    step(DVE.tensor_scalar_add(total[:], total[:], TOP_EPS), base)
                    step(DVE.reciprocal(top[:], total[:]), base)
                    DVE.tensor_tensor(gates[:], gates[:], per_token(top), ALU.mult).then_inc(gates_set, 1)
                if c == 9:
                    dve.wait_ge(gT_ps, n + 1)
                    wait(dve, rows_written, n * 16)
                    DVE.tensor_copy(gatesT[:], B[0:TI * E, 0:P]).then_inc(gT_set, 1)

            def fine(g, i):
                dve.wait_ge(hhi_set, g + 1)
                DVE.tensor_tensor(hid_lo[i % 4][:], hid[i % 2][:], hid_hi[i % 4][:].bitcast(fp32),
                                  ALU.subtract).then_inc(hlo_set, 1)

            def start():
                done[0] = 0
                dve.wait_ge(adj_in, 32)
                edges = adj_sb[:].unsqueeze(1).broadcast_to([P, TI, N])
                step(DVE.tensor_scalar(mask[:], edges, 0.0, None, ALU.is_gt), 0)
                step(DVE.tensor_scalar(no_edge[:], mask[:], -1.0, NEG, ALU.add, ALU.mult), 0)
                DVE.memset(probs[:], 0.0).then_inc(masks_set, 1)
                for c in range(CH):
                    if c == 2:
                        dve.wait_ge(hi_split, 2)
                        DVE.tensor_tensor(rw_lo[:], rw[:], rw_hi[:].bitcast(fp32), ALU.subtract)
                        DVE.tensor_tensor(w1_lo[:], w1_in, w1_hi[:].bitcast(fp32),
                                          ALU.subtract).then_inc(lo_split_dve, 1)
                    first_half(0, 0, c)
                dve.wait_ge(consts_set, 1)
                for c in range(CH):
                    second_half(0, 0, c)
                for c in range(CH):
                    first_half(1, 1, c)

            def body(b, par, second, first):
                dve.wait_ge(gate_loaded, (b + 1) * (16 * GATE_DMAS))
                for c in range(CH):
                    g, i = b * CH + c, par * CH + c
                    weight = c // FULL if c < PURE else E + c - PURE
                    dve.wait_ge(h3_done, g + 1)
                    wait(dve, hid_set, g - 1)
                    DVE.tensor_tensor(gated[i % 2][:], h3_ps[i % 2][:], gate[par][:, weight, :],
                                      ALU.mult).then_inc(gated_set, 1)
                    if not isinstance(g, int) or g > 0:
                        fine(g - 1, i - 1)
                    if second:
                        second_half(b + 1, 1 - par, c)
                    if first and c >= FIRST_HALF:
                        first_half(b + 2, par, c - FIRST_HALF)

            over_blocks(dve, start, body)
            fine(NB * CH - 1, 2 * CH - 1)

        @block.gpsimd
        def _(pool):
            def reciprocal_root(signal):
                POOL.tensor_tensor(rstd[:], var_eps[:], minus_half[:], ALU.pow).then_inc(signal, 1)

            def first_half(n, par, c):
                if c == 0:
                    pool.wait_ge(moments1, n + 1)
                    wait(pool, xn2_set, n)
                    reciprocal_root(rstd1)
                if c == 7:
                    pool.wait_ge(leaky_set, n + 1)
                    POOL.tensor_tensor(scores[:], scores[:], mask[:], ALU.mult).then_inc(pool_step, 1)
                    pool.wait_ge(pool_step, n + 4)
                    POOL.tensor_tensor(scores[:], scores[:], no_edge[:], ALU.add).then_inc(masked_set, 1)
                if c == 12:
                    pool.wait_ge(att_set, n + 1)
                    wait(pool, w2_done, (n - 1) * CH)
                    POOL.tensor_tensor(x2[par][:], x_in[par][:], att[:], ALU.add).then_inc(x2_set, 1)

            def second_half(n, par, c):
                if c == 0:
                    pool.wait_ge(moments2, n + 1)
                    reciprocal_root(rstd2)

            def start():
                POOL.memset(ident[:], 0.0).then_inc(pool_step, 1)
                pool.wait_ge(pool_step, 1)
                POOL.affine_select(out=ident[:], in_=ident[:], compare_op=ALU.not_equal, fill=1.0, base=0,
                                   pattern=[[-1, P]], channel_multiplier=1).then_inc(ident_set, 1)
                POOL.memset(earlier[:], 1.0).then_inc(pool_step, 1)
                pool.wait_ge(pool_step, 2)
                POOL.affine_select(out=earlier[:], in_=earlier[:], compare_op=ALU.is_gt, fill=0.0, base=0,
                                   pattern=[[0, TI], [1, E], [-1, E]], channel_multiplier=0).then_inc(consts_set, 1)
                POOL.memset(minus_half[:], -0.5).then_inc(pool_step, 1)
                pool.wait_ge(pool_step, 3)
                pool.wait_ge(masks_set, 1)
                for c in range(CH):
                    first_half(0, 0, c)
                pool.wait_ge(hi_split, 3)
                POOL.tensor_tensor(w3_lo[:], w3_in, w3_hi[:].bitcast(fp32), ALU.subtract).then_inc(lo_split_pool, 1)
                for c in range(CH):
                    second_half(0, 0, c)
                pool.wait_ge(hi_split, 4)
                POOL.tensor_tensor(w2_lo[:], w2_in, w2_hi[:].bitcast(fp32), ALU.subtract).then_inc(lo_split_pool, 1)
                for c in range(CH):
                    first_half(1, 1, c)

            def body(b, par, second, first):
                for c in range(CH):
                    g, i = b * CH + c, par * CH + c
                    pool.wait_ge(act_set, g + 1)
                    pool.wait_ge(gated_set, g + 1)
                    wait(pool, hlo_set, g - 1)
                    POOL.tensor_tensor(hid[i % 2][:], act[i % 2][:], gated[i % 2][:], ALU.mult).then_inc(hid_set, 1)
                    if second:
                        second_half(b + 1, 1 - par, c)
                    if first and c >= FIRST_HALF:
                        first_half(b + 2, par, c - FIRST_HALF)

            over_blocks(pool, start, body)


def hidden_order():
    whole = [e * H + k for e in range(E) for k in range(FULL * P)]
    rest = [e * H + FULL * P + k for e in range(E) for k in range(REST)]
    return whole + rest


def kernel(x, adj, L0_gnn_W1, L0_gnn_W2, L0_gnn_W3, L0_ffn_router_w, L0_ffn_w1, L0_ffn_w2, L0_ffn_w3):
    import numpy as np
    import concourse.bacc as bacc
    from concourse.bass_utils import run_bass_kernel_spmd

    def a(v):
        return np.asarray(v)

    order = hidden_order()
    pad = CH * P - len(order)
    router = np.pad(a(L0_ffn_router_w).T, ((0, 0), (0, P - E)))
    w1T = np.pad(a(L0_ffn_w1).reshape(E * H, C)[order].T, ((0, 0), (0, pad)))
    w3T = np.pad(a(L0_ffn_w3).reshape(E * H, C)[order].T, ((0, 0), (0, pad)))
    w2 = np.pad(a(L0_ffn_w2).transpose(0, 2, 1).reshape(E * H, C)[order], ((0, pad), (0, 0)))
    given = {
        "x_dram": a(x).reshape(T, C), "adj_dram": a(adj), "gnn_w1T_dram": a(L0_gnn_W1).T,
        "gnn_w2T_dram": a(L0_gnn_W2).T, "gnn_w3_dram": a(L0_gnn_W3), "router_dram": router,
        "w1T_dram": w1T, "w3T_dram": w3T, "w2_dram": w2,
    }
    given = {k: np.ascontiguousarray(v) for k, v in given.items()}

    nc = bacc.Bacc("TRN2", target_bir_lowering=False, num_devices=1)
    args = [nc.dram_tensor(k, v.shape, mybir.dt.from_np(v.dtype), kind="ExternalInput").ap()
            for k, v in given.items()]
    args.append(nc.dram_tensor("outT_dram", (C, T), mybir.dt.float32, kind="ExternalOutput").ap())
    bass_gnn_moe_kernel(nc, *args)
    got = run_bass_kernel_spmd(nc, [given], core_ids=[0]).results[0]["outT_dram"]
    return np.ascontiguousarray(got.T).reshape(BATCH, N, C)
```

```python
from contextlib import ExitStack

import concourse.bass as bass
from concourse import mybir


BATCH, N, C = 128, 64, 128
E, H = 8, 341
P = 128
T = BATCH * N
BT = 512
NB = T // BT
TI = BT // P
FULL = H // P
REST = H - FULL * P
PURE = E * FULL
MIXED = -(-E * REST // P)
CH = PURE + MIXED
LAG = 3
ALPHA, NEG, EPS, TOP_EPS = 0.2, 1e12, 1e-5, 1e-9

SEGMENTS = []
for _k in range(MIXED):
    _p = 0
    while _p < P:
        _e = min((_k * P + _p) // REST, E - 1)
        _end = P if _e == E - 1 else min(P, (_e + 1) * REST - _k * P)
        SEGMENTS.append((_k, _p, _end, _e))
        _p = _end
SOON = 4
LATE_DMAS = 1 + len(SEGMENTS)



def bass_gnn_moe_kernel(nc, x, adj, gnn_w1T, gnn_w2T, gnn_w3, routerT, w1T, w3T, w2, outT):
    fp32, fp32r, i32 = mybir.dt.float32, mybir.dt.float32r, mybir.dt.int32
    ALU, ACT, X = mybir.AluOpType, mybir.ActivationFunctionType, mybir.AxisListType.X
    PE, DVE, SCA, POOL, SP = nc.tensor, nc.vector, nc.scalar, nc.gpsimd, nc.sync

    x_blocks = x.rearrange("(b t p) c -> p b t c", t=TI, p=P)
    gate_rows = [nc.dram_tensor(f"gate_rows{i}", (E, BT), fp32).ap() for i in range(2)]

    with ExitStack() as ctx:
        def sb(name, shape, dt=fp32):
            return ctx.enter_context(nc.sbuf_tensor(name, shape, dt))

        def pair(name, shape, dt=fp32, n=2):
            return [sb(f"{name}{i}", shape, dt) for i in range(n)]

        def bank(name):
            return ctx.enter_context(nc.psum_tensor(name, [P, BT], fp32))

        def sem(name):
            return ctx.enter_context(nc.semaphore(name))

        ident = sb("ident", [P, P])
        adj_sb = sb("adj_sb", [P, N], i32)
        mask = sb("mask", [P, TI, N])
        no_edge = sb("no_edge", [P, TI, N])
        earlier = sb("earlier", [P, TI, E, E])
        minus_half, eps = sb("minus_half", [P, TI]), sb("eps", [P, TI])
        g1T, g2T, g3 = sb("g1T", [P, C]), sb("g2T", [P, C]), sb("g3", [P, C])
        scores_w = sb("scores_w", [P, C])
        rw = sb("rw", [P, P])
        rw_hi, rw_lo = sb("rw_hi", [P, P], fp32r), sb("rw_lo", [P, P], fp32r)
        w1_hi, w1_lo = sb("w1_hi", [P, CH, P], fp32r), sb("w1_lo", [P, CH, P], fp32r)
        w3_hi, w3_lo = sb("w3_hi", [P, CH, P], fp32r), sb("w3_lo", [P, CH, P], fp32r)
        w2_hi, w2_lo = sb("w2_hi", [P, CH, P], fp32r), sb("w2_lo", [P, CH, P], fp32r)
        gate = pair("gate", [P, E + MIXED, BT])
        w1_in = gate[1][:, 0:6, :].rearrange("p a b -> p (a b)")[:, 0:CH * P].rearrange("p (c k) -> p c k", k=P)
        w3_in = gate[1][:, 6:12, :].rearrange("p a b -> p (a b)")[:, 0:CH * P].rearrange("p (c k) -> p c k", k=P)
        w2_in = gate[0][:, 0:6, :].rearrange("p a b -> p (a b)")[:, 0:CH * P].rearrange("p (c k) -> p c k", k=P)

        x_in = pair("x_in", [P, TI, C])
        stats = sb("stats", [P, TI, 6])
        apart, squares = sb("apart", [P, TI]), sb("squares", [P, TI])
        mean, var_eps, rstd = sb("mean", [P, TI]), sb("var_eps", [P, TI]), sb("rstd", [P, TI])
        xn = sb("xn", [P, TI, C])
        xnT = sb("xnT", [P, BT])
        qT = sb("qT", [P, BT])
        v = sb("v", [P, TI, C])
        small_e = sb("small_e", [P, TI, N])
        scores = sb("scores", [P, TI, N])
        row_max = sb("row_max", [P, TI])
        probs = sb("probs", [P, TI, P])
        row_sum = sb("row_sum", [P, TI])
        row_scale = sb("row_scale", [P, TI])
        probsT = sb("probsT", [P, TI, P])
        att = sb("att", [P, TI, C])
        x2 = pair("x2", [P, TI, C])
        mean2, var_eps2, rstd2 = sb("mean2", [P, TI]), sb("var_eps2", [P, TI]), sb("rstd2", [P, TI])
        xn2 = sb("xn2", [P, TI, C])
        xT_hi, xT_lo = pair("xT_hi", [P, BT], fp32r), pair("xT_lo", [P, BT], fp32r)
        logitsT = sb("logitsT", [P, BT])
        logits = sb("logits", [P, TI, E])
        top = sb("top", [P, TI])
        shifted = sb("shifted", [P, TI, E])
        expo = sb("expo", [P, TI, E])
        total = sb("total", [P, TI])
        prob = sb("prob", [P, TI, E])
        above = sb("above", [P, TI, E, E])
        tied = sb("tied", [P, TI, E, E])
        rank = sb("rank", [P, TI, E])
        gates = sb("gates", [P, TI, E])
        gatesT = sb("gatesT", [TI * E, P])
        act = pair("act", [P, BT])
        gated = pair("gated", [P, BT])
        hid = pair("hid", [P, BT])
        hid_hi, hid_lo = pair("hid_hi", [P, BT], fp32r, 4), pair("hid_lo", [P, BT], fp32r, 4)
        y_out = sb("y_out", [P, BT])

        h1_ps, h3_ps = [bank("h1_ps0"), bank("h1_ps1")], [bank("h3_ps0"), bank("h3_ps1")]
        y_ps = bank("y_ps")
        A, B, D = bank("att_ps0"), bank("att_ps1"), bank("router_ps")

        gnn_in, adj_in, x_arrived = sem("gnn_in"), sem("adj_in"), sem("x_arrived")
        w1_arrived, w3_arrived, w2_arrived = sem("w1_arrived"), sem("w3_arrived"), sem("w2_arrived")
        pool_step, ident_set, consts_set, masks_set = (sem(n) for n in ("pool_step", "ident_set", "consts_set", "masks_set"))
        wprod_ps, wprod_set, edges_set = sem("wprod_ps"), sem("wprod_set"), sem("edges_set")
        hi_split, lo_split_dve, lo_split_pool = sem("hi_split"), sem("lo_split_dve"), sem("lo_split_pool")
        att_step = sem("att_step")
        moments_set, rstd_set, xn_set, xT_ps, xT_set = (sem(n) for n in ("moments_set", "rstd_set", "xn_set", "xT_ps", "xT_set"))
        q_ps, q_set, v_ps, v_set, e_ps = (sem(n) for n in ("q_ps", "q_set", "v_ps", "v_set", "e_ps"))
        small_set, leaky_set, kept_set, masked_set, shifted_set = (sem(n) for n in ("small_set", "leaky_set", "kept_set", "masked_set", "shifted_set"))
        probs_set, scale_set, pT_ps, pT_set, pv_ps = (sem(n) for n in ("probs_set", "scale_set", "pT_ps", "pT_set", "pv_ps"))
        att_set, x2_set = sem("att_set"), sem("x2_set")
        router_step = sem("router_step")
        moments2_set, rstd2_set, xn2_set, x2T_ps, xhi_set = (sem(n) for n in ("moments2_set", "rstd2_set", "xn2_set", "x2T_ps", "xhi_set"))
        xlo_set, lgT_ps, lgT_set, lg_ps, lg_shifted = (sem(n) for n in ("xlo_set", "lgT_ps", "lgT_set", "lg_ps", "lg_shifted"))
        lg_exp, inverse_set, gates_set, gT_ps, gT_set = (sem(n) for n in ("lg_exp", "inverse_set", "gates_set", "gT_ps", "gT_set"))
        rows_written, gate_soon, gate_late = sem("rows_written"), sem("gate_soon"), sem("gate_late")
        h1_done, h3_done, act_set, gated_set = (sem(n) for n in ("h1_done", "h3_done", "act_set", "gated_set"))
        hid_set, hhi_set, hlo_set, w2_done = (sem(n) for n in ("hid_set", "hhi_set", "hlo_set", "w2_done"))
        y_set, out_stored = sem("y_set"), sem("out_stored")

        block = ctx.enter_context(nc.Block())

        def wait(eng, s, count):
            if not isinstance(count, int) or count > 0:
                eng.wait_ge(s, count)

        def over_blocks(eng, start, prepare, multiply):
            def turn(b, par, chunks=True, next_block=True, block_after=True):
                for c in range(CH):
                    if chunks:
                        multiply(b, par, c)
                    if next_block:
                        prepare(b + 1, 1 - par, CH + c)
                    if block_after:
                        prepare(b + 2, par, c)

            start()
            turn(-2, 0, chunks=False, next_block=False)
            turn(-1, 1, chunks=False)
            turn(0, 0)
            with eng.Fori(0, (NB - 4) // 2) as i:
                turn(i * 2 + 1, 1)
                turn(i * 2 + 2, 0)
            turn(NB - 3, 1)
            turn(NB - 2, 0, block_after=False)
            turn(NB - 1, 1, next_block=False, block_after=False)

        @block.sync
        def _(sp):
            def load_x(n, par):
                wait(sp, moments_set, n)
                sp.dma_start(x_in[par][:], x_blocks[:, n] if isinstance(n, int) else
                             x_blocks[:, bass.ds(n, 1)].rearrange("p b t c -> p (b t) c")).then_inc(x_arrived, 16)

            def load_gates(n, par):
                sp.wait_ge(gT_set, n + 1)
                sp.dma_start(gate_rows[par].rearrange("e (t p) -> t e p", t=TI), gatesT[:]).then_inc(rows_written, 16)
                sp.wait_ge(rows_written, n * 16 + 16)
                for e0, e1, signal in ((0, SOON, gate_soon), (SOON, E, gate_late)):
                    sp.dma_start(gate[par][:, e0:e1, :].rearrange("p e t -> p (e t)"),
                                 gate_rows[par][e0:e1].rearrange("e t -> (e t)").partition_broadcast(P)).then_inc(signal, 16)
                for k, p0, p1, e in SEGMENTS:
                    sp.dma_start(gate[par][p0:p1, E + k, :],
                                 gate_rows[par][e].partition_broadcast(p1 - p0)).then_inc(gate_late, 16)

            def store_out(n):
                sp.wait_ge(y_set, n + 1)
                sp.dma_start(outT[:, bass.ds(n * BT, BT)], y_out[:]).then_inc(out_stored, 16)

            def start():
                load_x(0, 0)
                sp.dma_start(g1T[:], gnn_w1T).then_inc(gnn_in, 16)
                sp.dma_start(g2T[:], gnn_w2T).then_inc(gnn_in, 16)
                sp.dma_start(g3[:], gnn_w3).then_inc(gnn_in, 16)
                sp.dma_start(rw[:], routerT).then_inc(gnn_in, 16)
                sp.dma_start(adj_sb[0:N, :], adj).then_inc(adj_in, 16)
                sp.dma_start(adj_sb[N:P, :], adj).then_inc(adj_in, 16)
                sp.dma_start(w1_in, w1T.rearrange("c (k h) -> c k h", h=P)).then_inc(w1_arrived, 16)
                sp.dma_start(w3_in, w3T.rearrange("c (k h) -> c k h", h=P)).then_inc(w3_arrived, 16)
                sp.dma_start(w2_in, w2.rearrange("(k h) c -> h k c", h=P)).then_inc(w2_arrived, 16)
                load_x(1, 1)
                load_x(2, 0)
                sp.wait_ge(hi_split, 4)
                sp.wait_ge(lo_split_dve, 1)
                sp.wait_ge(lo_split_pool, 2)
                load_gates(0, 0)

            def turn(b, par, load=True, gates=True):
                if load:
                    load_x(b + 3, 1 - par)
                if not isinstance(b, int) or b > 0:
                    store_out(b - 1)
                if gates:
                    load_gates(b + 1, 1 - par)

            start()
            turn(0, 0)
            with sp.Fori(0, (NB - 4) // 2) as i:
                turn(i * 2 + 1, 1)
                turn(i * 2 + 2, 0)
            turn(NB - 3, 1, load=False)
            turn(NB - 2, 0, load=False)
            turn(NB - 1, 1, load=False, gates=False)
            store_out(NB - 1)
            sp.wait_ge(out_stored, NB * 16)

        @block.tensor
        def _(pe):
            def split_product(out, hi_w, lo_w, hi_x, lo_x, start=True, stop=True):
                PE.matmul(out, hi_w, hi_x, start=start, stop=False, skip_group_check=True)
                PE.matmul(out, hi_w, lo_x, start=False, stop=False, skip_group_check=True)
                return PE.matmul(out, lo_w, hi_x, start=False, stop=stop, skip_group_check=True)

            def prepare(n, par, k):
                if k == 5:
                    pe.wait_ge(xn_set, n + 1)
                    wait(pe, xlo_set, n)
                    for t in range(TI):
                        last = PE.transpose(A[:, t * P:(t + 1) * P], xn[:, t, :], ident[:])
                    last.then_inc(xT_ps, 1)
                if k == 7:
                    pe.wait_ge(xT_set, n + 1)
                    wait(pe, att_set, n)
                    PE.matmul(B[:], scores_w[:], xnT[:], start=True, stop=True).then_inc(q_ps, 1)
                if k == 8:
                    for t in range(TI):
                        last = PE.matmul(A[:, t * P:(t + 1) * P], xnT[:, t * P:(t + 1) * P], g3[:],
                                         start=True, stop=True, skip_group_check=True)
                    last.then_inc(v_ps, 1)
                if k == 9:
                    pe.wait_ge(q_set, n + 1)
                    for t in range(TI):
                        for g in range(2):
                            at = t * P + g * N
                            last = PE.matmul(B[g * N:(g + 1) * N, t * N:(t + 1) * N], qT[:, at:at + N],
                                             xnT[:, at:at + N], start=True, stop=True, skip_group_check=True)
                    last.then_inc(e_ps, 1)
                if k == 14:
                    pe.wait_ge(probs_set, n + 1)
                    pe.wait_ge(v_set, n + 1)
                    for t in range(TI):
                        last = PE.transpose(A[:, t * P:(t + 1) * P], probs[:, t, :], ident[:])
                    last.then_inc(pT_ps, 1)
                if k == 16:
                    pe.wait_ge(pT_set, n + 1)
                    for t in range(TI):
                        last = PE.matmul(B[:, t * P:(t + 1) * P], probsT[:, t, :], v[:, t, :],
                                         start=True, stop=True, skip_group_check=True)
                    last.then_inc(pv_ps, 1)
                if k == 24:
                    pe.wait_ge(xn2_set, n + 1)
                    for t in range(TI):
                        last = PE.transpose(A[:, t * P:(t + 1) * P], xn2[:, t, :], ident[:])
                    last.then_inc(x2T_ps, 1)
                if k == 26:
                    pe.wait_ge(xlo_set, n + 1)
                    wait(pe, gT_set, n)
                    split_product(D[:], rw_hi[:], rw_lo[:], xT_hi[par][:], xT_lo[par][:]).then_inc(lgT_ps, 1)
                if k == 28:
                    pe.wait_ge(lgT_set, n + 1)
                    for t in range(TI):
                        last = PE.transpose(D[:, t * P:(t + 1) * P], logitsT[:, t * P:(t + 1) * P], ident[:])
                    last.then_inc(lg_ps, 1)
                if k == 35:
                    pe.wait_ge(gates_set, n + 1)
                    PE.transpose(D[0:TI * E, 0:P], gates[:].rearrange("p t e -> p (t e)"),
                                 ident[:]).then_inc(gT_ps, 1)

            def start():
                pe.wait_ge(gnn_in, 64)
                PE.matmul(B[:, 0:C], g1T[:], g2T[:], start=True, stop=True).then_inc(wprod_ps, 1)
                pe.wait_ge(ident_set, 1)
                pe.wait_ge(wprod_set, 1)

            def multiply(b, par, c):
                g, i = b * CH + c, par * CH + c
                if c == 0:
                    pe.wait_ge(xlo_set, b + 1)
                    if isinstance(b, int) and b == 0:
                        pe.wait_ge(lo_split_dve, 1)
                        pe.wait_ge(lo_split_pool, 1)
                wait(pe, act_set, g - 1)
                split_product(h1_ps[i % 2][:], w1_hi[:, c, :], w1_lo[:, c, :],
                              xT_hi[par][:], xT_lo[par][:]).then_inc(h1_done, 1)
                wait(pe, gated_set, g - 1)
                split_product(h3_ps[i % 2][:], w3_hi[:, c, :], w3_lo[:, c, :],
                              xT_hi[par][:], xT_lo[par][:]).then_inc(h3_done, 1)
                if c >= LAG:
                    pe.wait_ge(hlo_set, g - LAG + 1)
                    if c == LAG:
                        if isinstance(b, int) and b == 0:
                            pe.wait_ge(lo_split_pool, 2)
                        wait(pe, y_set, b)
                    split_product(y_ps[:], w2_hi[:, c - LAG, :], w2_lo[:, c - LAG, :],
                                  hid_hi[(i - LAG) % 4][:], hid_lo[(i - LAG) % 4][:],
                                  start=(c == LAG), stop=False).then_inc(w2_done, 1)
                    if c == LAG:
                        for t in range(TI):
                            PE.matmul(y_ps[:, t * P:(t + 1) * P], x2[par][:, t, :], ident[:],
                                      start=False, stop=False, skip_group_check=True)
                elif not isinstance(b, int) or b > 0:
                    tail_product(b, par, c)

            def tail_product(b, par, c):
                g, i = b * CH + c - LAG, (par * CH + c - LAG) % 4
                k = CH - LAG + c
                pe.wait_ge(hlo_set, g + 1)
                split_product(y_ps[:], w2_hi[:, k, :], w2_lo[:, k, :], hid_hi[i][:], hid_lo[i][:],
                              start=False, stop=(k == CH - 1)).then_inc(w2_done, 1)

            over_blocks(pe, start, prepare, multiply)
            for c in range(LAG):
                tail_product(NB, 0, c)

        @block.scalar
        def _(sc):
            def prepare(n, par, k):
                if k == 6:
                    sc.wait_ge(xT_ps, n + 1)
                    SCA.activation(xnT[:], A[:], ACT.Copy).then_inc(xT_set, 1)
                if k == 9:
                    sc.wait_ge(v_ps, n + 1)
                    SCA.activation(v[:].rearrange("p t c -> p (t c)"), A[:], ACT.Copy).then_inc(v_set, 1)
                if k == 10:
                    sc.wait_ge(e_ps, n + 1)
                    SCA.activation(small_e[:].rearrange("p t c -> p (t c)"), B[:, 0:TI * N], ACT.Copy,
                                   scale=ALPHA).then_inc(small_set, 1)
                if k == 13:
                    sc.wait_ge(shifted_set, n + 1)
                    for g in range(2):
                        at = slice(g * N, (g + 1) * N)
                        last = SCA.activation(probs[at, :, at], scores[at, :, :], ACT.Exp)
                    last.then_inc(probs_set, 1)
                if k == 15:
                    sc.wait_ge(pT_ps, n + 1)
                    SCA.activation(probsT[:].rearrange("p t m -> p (t m)"), A[:], ACT.Copy).then_inc(pT_set, 1)
                if k == 17:
                    sc.wait_ge(pv_ps, n + 1)
                    sc.wait_ge(scale_set, n + 1)
                    for t in range(TI):
                        last = SCA.activation(att[:, t, :], B[:, t * P:(t + 1) * P], ACT.Relu,
                                              scale=row_scale[:, t:t + 1])
                    last.then_inc(att_set, 1)
                if k == 25:
                    sc.wait_ge(x2T_ps, n + 1)
                    wait(sc, h3_done, (n - 1) * CH)
                    SCA.activation(xT_hi[par][:], A[:], ACT.Copy).then_inc(xhi_set, 1)
                if k == 27:
                    sc.wait_ge(lgT_ps, n + 1)
                    SCA.activation(logitsT[:], D[:], ACT.Copy).then_inc(lgT_set, 1)
                if k == 30:
                    sc.wait_ge(lg_shifted, n + 1)
                    SCA.activation(expo[:].rearrange("p t e -> p (t e)"),
                                   shifted[:].rearrange("p t e -> p (t e)"), ACT.Exp).then_inc(lg_exp, 1)
                if isinstance(n, int) and n == 0 and k in WEIGHTS_AT:
                    w_in, hi, arrived = WEIGHTS_AT[k]
                    sc.wait_ge(arrived, 16)
                    SCA.activation(hi[:], w_in, ACT.Copy).then_inc(hi_split, 1)

            WEIGHTS_AT = {6: (w1_in, w1_hi, w1_arrived), 15: (w3_in, w3_hi, w3_arrived),
                          17: (w2_in, w2_hi, w2_arrived)}

            def coarse(g, i):
                sc.wait_ge(hid_set, g + 1)
                wait(sc, w2_done, g - 3)
                SCA.activation(hid_hi[i % 4][:], hid[i % 2][:], ACT.Copy).then_inc(hhi_set, 1)

            def start():
                sc.wait_ge(wprod_ps, 1)
                SCA.activation(scores_w[:], B[:, 0:C], ACT.Copy).then_inc(wprod_set, 1)
                SCA.activation(rw_hi[:], rw[:], ACT.Copy).then_inc(hi_split, 1)

            def multiply(b, par, c):
                g, i = b * CH + c, par * CH + c
                sc.wait_ge(h1_done, g + 1)
                wait(sc, hid_set, g - 1)
                SCA.activation(act[i % 2][:], h1_ps[i % 2][:], ACT.Silu).then_inc(act_set, 1)
                if not isinstance(g, int) or g > 0:
                    coarse(g - 1, i - 1)
                if c == LAG and (not isinstance(b, int) or b > 0):
                    result(b - 1)

            def result(n):
                sc.wait_ge(w2_done, n * CH + CH)
                wait(sc, out_stored, n * 16)
                SCA.activation(y_out[:], y_ps[:], ACT.Copy).then_inc(y_set, 1)

            over_blocks(sc, start, prepare, multiply)
            coarse(NB * CH - 1, 2 * CH - 1)
            result(NB - 1)

        @block.vector
        def _(dve):
            ATT_STEPS, ROUTER_STEPS = 6, 16

            def att(instruction, n, j):
                instruction.then_inc(att_step, 1)
                dve.wait_ge(att_step, n * ATT_STEPS + j)

            def router(instruction, n, j):
                instruction.then_inc(router_step, 1)
                dve.wait_ge(router_step, n * ROUTER_STEPS + j)

            def even_odd(source):
                for t in range(TI):
                    last = DVE.bn_stats(stats[:, t, :], source[:, t, :])
                return last

            def moments(mean, var_eps, step, n):
                DVE.tensor_tensor(mean[:], stats[:, :, 1], stats[:, :, 4], ALU.add)
                DVE.tensor_tensor(apart[:], stats[:, :, 1], stats[:, :, 4], ALU.subtract)
                step(DVE.tensor_tensor(squares[:], stats[:, :, 2], stats[:, :, 5], ALU.add), n, 2)
                DVE.tensor_scalar(mean[:], mean[:], 0.5, None, ALU.mult)
                step(DVE.tensor_tensor(apart[:], apart[:], apart[:], ALU.mult), n, 3)
                step(DVE.scalar_tensor_tensor(squares[:], apart[:], C / 4, squares[:], ALU.mult, ALU.add), n, 4)
                return DVE.tensor_scalar(var_eps[:], squares[:], 1 / C, EPS, ALU.mult, ALU.add)

            def normalise(out, source, mean, rstd, tiles):
                for t in tiles:
                    last = DVE.tensor_scalar(out[:, t, :], source[:, t, :], mean[:, t:t + 1],
                                             rstd[:, t:t + 1], ALU.subtract, ALU.mult)
                return last

            def per_token(a, m):
                return a[:].unsqueeze(2).broadcast_to([P, TI, m])

            def prepare(n, par, k):
                if k == 0:
                    dve.wait_ge(x_arrived, n * 16 + 16)
                    even_odd(x_in[par]).then_inc(att_step, 1)
                if k == 1:
                    dve.wait_ge(att_step, n * ATT_STEPS + 1)
                    moments(mean, var_eps, att, n).then_inc(moments_set, 1)
                if k == 3:
                    dve.wait_ge(rstd_set, n + 1)
                    wait(dve, xT_ps, n)
                    normalise(xn, x_in[par], mean, rstd, (0, 1))
                if k == 4:
                    normalise(xn, x_in[par], mean, rstd, (2, 3)).then_inc(xn_set, 1)
                if k == 8:
                    dve.wait_ge(q_ps, n + 1)
                    DVE.tensor_copy(qT[:], B[:]).then_inc(q_set, 1)
                if k == 10:
                    dve.wait_ge(small_set, n + 1)
                    DVE.tensor_tensor(scores[:].rearrange("p t m -> p (t m)"), B[:, 0:TI * N],
                                      small_e[:].rearrange("p t m -> p (t m)"), ALU.max).then_inc(leaky_set, 1)
                if k == 12:
                    dve.wait_ge(masked_set, n + 1)
                    att(DVE.reduce_max(row_max[:], scores[:], axis=X), n, 5)
                    DVE.tensor_tensor(scores[:], scores[:], per_token(row_max, N), ALU.subtract).then_inc(shifted_set, 1)
                if k == 14:
                    dve.wait_ge(probs_set, n + 1)
                    att(DVE.reduce_sum(row_sum[:], probs[:], axis=X), n, 6)
                    DVE.reciprocal(row_scale[:], row_sum[:]).then_inc(scale_set, 1)
                if k == 19:
                    dve.wait_ge(x2_set, n + 1)
                    even_odd(x2[par]).then_inc(router_step, 1)
                if k == 20:
                    dve.wait_ge(router_step, n * ROUTER_STEPS + 1)
                    moments(mean2, var_eps2, router, n).then_inc(moments2_set, 1)
                if k == 22:
                    dve.wait_ge(rstd2_set, n + 1)
                    wait(dve, x2T_ps, n)
                    normalise(xn2, x2[par], mean2, rstd2, (0, 1))
                if k == 23:
                    normalise(xn2, x2[par], mean2, rstd2, (2, 3)).then_inc(xn2_set, 1)
                if k == 25:
                    dve.wait_ge(xhi_set, n + 1)
                    DVE.tensor_tensor(xT_lo[par][:], A[:], xT_hi[par][:].bitcast(fp32),
                                      ALU.subtract).then_inc(xlo_set, 1)
                if k == 29:
                    dve.wait_ge(lg_ps, n + 1)
                    router(DVE.tensor_copy(logits[:], D[:].rearrange("p (t e) -> p t e", t=TI)[:, :, 0:E]), n, 5)
                    router(DVE.reduce_max(top[:], logits[:], axis=X), n, 6)
                    DVE.tensor_tensor(shifted[:], logits[:], per_token(top, E), ALU.subtract).then_inc(lg_shifted, 1)
                if k == 31:
                    dve.wait_ge(lg_exp, n + 1)
                    router(DVE.reduce_sum(total[:], expo[:], axis=X), n, 7)
                    router(DVE.reciprocal(top[:], total[:]), n, 8)
                    router(DVE.tensor_tensor(prob[:], expo[:], per_token(top, E), ALU.mult), n, 9)
                this = prob[:].unsqueeze(3).broadcast_to([P, TI, E, E])
                other = prob[:].unsqueeze(2).broadcast_to([P, TI, E, E])
                if k == 32:
                    DVE.tensor_tensor(above[:], other, this, ALU.is_gt)
                    router(DVE.tensor_tensor(tied[:], other, this, ALU.is_equal), n, 10)
                    DVE.tensor_tensor(tied[:], tied[:], earlier[:], ALU.mult).then_inc(router_step, 1)
                if k == 33:
                    dve.wait_ge(router_step, n * ROUTER_STEPS + 11)
                    router(DVE.tensor_tensor(above[:], above[:], tied[:], ALU.add), n, 12)
                    router(DVE.reduce_sum(rank[:], above[:], axis=X), n, 13)
                    router(DVE.scalar_tensor_tensor(gates[:], rank[:], 1.5, prob[:], ALU.is_lt, ALU.mult), n, 14)
                if k == 34:
                    router(DVE.reduce_sum(total[:], gates[:], axis=X), n, 15)
                    router(DVE.tensor_scalar_add(total[:], total[:], TOP_EPS), n, 16)
                    DVE.reciprocal(top[:], total[:]).then_inc(inverse_set, 1)
                    dve.wait_ge(inverse_set, n + 1)
                    DVE.tensor_tensor(gates[:], gates[:], per_token(top, E), ALU.mult).then_inc(gates_set, 1)
                if k == 36:
                    dve.wait_ge(gT_ps, n + 1)
                    wait(dve, rows_written, n * 16)
                    DVE.tensor_copy(gatesT[:], D[0:TI * E, 0:P]).then_inc(gT_set, 1)
                if isinstance(n, int) and n == 0 and k == 12:
                    dve.wait_ge(hi_split, 2)
                    DVE.tensor_tensor(rw_lo[:], rw[:], rw_hi[:].bitcast(fp32), ALU.subtract)
                    DVE.tensor_tensor(w1_lo[:], w1_in, w1_hi[:].bitcast(fp32), ALU.subtract).then_inc(lo_split_dve, 1)

            def fine(g, i):
                dve.wait_ge(hhi_set, g + 1)
                DVE.tensor_tensor(hid_lo[i % 4][:], hid[i % 2][:], hid_hi[i % 4][:].bitcast(fp32),
                                  ALU.subtract).then_inc(hlo_set, 1)

            def start():
                dve.wait_ge(adj_in, 32)
                DVE.tensor_scalar(mask[:], adj_sb[:].unsqueeze(1).broadcast_to([P, TI, N]), 0.0, None,
                                  ALU.is_gt).then_inc(edges_set, 1)
                dve.wait_ge(edges_set, 1)
                DVE.tensor_scalar(no_edge[:], mask[:], -1.0, NEG, ALU.add, ALU.mult)
                DVE.memset(probs[:], 0.0).then_inc(masks_set, 1)
                dve.wait_ge(consts_set, 1)

            def multiply(b, par, c):
                g, i = b * CH + c, par * CH + c
                weight = c // FULL if c < PURE else E + c - PURE
                if c == 0:
                    dve.wait_ge(gate_soon, b * 16 + 16)
                if c == SOON * FULL:
                    dve.wait_ge(gate_late, (b + 1) * (16 * LATE_DMAS))
                dve.wait_ge(h3_done, g + 1)
                wait(dve, hid_set, g - 1)
                DVE.tensor_tensor(gated[i % 2][:], h3_ps[i % 2][:], gate[par][:, weight, :],
                                  ALU.mult).then_inc(gated_set, 1)
                if not isinstance(g, int) or g > 0:
                    fine(g - 1, i - 1)

            over_blocks(dve, start, prepare, multiply)
            fine(NB * CH - 1, 2 * CH - 1)

        @block.gpsimd
        def _(pool):
            def prepare(n, par, k):
                if k == 2:
                    pool.wait_ge(moments_set, n + 1)
                    POOL.tensor_tensor(rstd[:], var_eps[:], minus_half[:], ALU.pow).then_inc(rstd_set, 1)
                if k == 11:
                    pool.wait_ge(leaky_set, n + 1)
                    POOL.tensor_tensor(scores[:], scores[:], mask[:], ALU.mult).then_inc(kept_set, 1)
                    pool.wait_ge(kept_set, n + 1)
                    POOL.tensor_tensor(scores[:], scores[:], no_edge[:], ALU.add).then_inc(masked_set, 1)
                if k == 18:
                    pool.wait_ge(att_set, n + 1)
                    wait(pool, w2_done, (n - 2) * CH + 2 if not isinstance(n, int) or n >= 2 else 0)
                    POOL.tensor_tensor(x2[par][:], x_in[par][:], att[:], ALU.add).then_inc(x2_set, 1)
                if k == 21:
                    pool.wait_ge(moments2_set, n + 1)
                    POOL.tensor_tensor(rstd2[:], var_eps2[:], minus_half[:], ALU.pow).then_inc(rstd2_set, 1)
                if isinstance(n, int) and n == 0 and k == 18:
                    pool.wait_ge(hi_split, 3)
                    POOL.tensor_tensor(w3_lo[:], w3_in, w3_hi[:].bitcast(fp32), ALU.subtract).then_inc(lo_split_pool, 1)
                if isinstance(n, int) and n == 0 and k == 21:
                    pool.wait_ge(hi_split, 4)
                    POOL.tensor_tensor(w2_lo[:], w2_in, w2_hi[:].bitcast(fp32), ALU.subtract).then_inc(lo_split_pool, 1)

            def start():
                POOL.memset(ident[:], 0.0).then_inc(pool_step, 1)
                pool.wait_ge(pool_step, 1)
                POOL.affine_select(out=ident[:], in_=ident[:], compare_op=ALU.not_equal, fill=1.0, base=0,
                                   pattern=[[-1, P]], channel_multiplier=1).then_inc(ident_set, 1)
                POOL.memset(earlier[:], 1.0).then_inc(pool_step, 1)
                pool.wait_ge(pool_step, 2)
                POOL.affine_select(out=earlier[:], in_=earlier[:], compare_op=ALU.is_gt, fill=0.0, base=0,
                                   pattern=[[0, TI], [1, E], [-1, E]], channel_multiplier=0).then_inc(consts_set, 1)
                POOL.memset(minus_half[:], -0.5).then_inc(pool_step, 1)
                pool.wait_ge(pool_step, 3)
                pool.wait_ge(masks_set, 1)

            def multiply(b, par, c):
                g, i = b * CH + c, par * CH + c
                pool.wait_ge(act_set, g + 1)
                pool.wait_ge(gated_set, g + 1)
                wait(pool, hlo_set, g - 1)
                POOL.tensor_tensor(hid[i % 2][:], act[i % 2][:], gated[i % 2][:], ALU.mult).then_inc(hid_set, 1)

            over_blocks(pool, start, prepare, multiply)


def hidden_order():
    whole = [e * H + k for e in range(E) for k in range(FULL * P)]
    rest = [e * H + FULL * P + k for e in range(E) for k in range(REST)]
    return whole + rest


def kernel(x, adj, L0_gnn_W1, L0_gnn_W2, L0_gnn_W3, L0_ffn_router_w, L0_ffn_w1, L0_ffn_w2, L0_ffn_w3):
    import numpy as np
    import concourse.bacc as bacc
    from concourse.bass_utils import run_bass_kernel_spmd

    def a(v):
        return np.asarray(v)

    order = hidden_order()
    pad = CH * P - len(order)
    router = np.pad(a(L0_ffn_router_w).T, ((0, 0), (0, P - E)))
    w1T = np.pad(a(L0_ffn_w1).reshape(E * H, C)[order].T, ((0, 0), (0, pad)))
    w3T = np.pad(a(L0_ffn_w3).reshape(E * H, C)[order].T, ((0, 0), (0, pad)))
    w2 = np.pad(a(L0_ffn_w2).transpose(0, 2, 1).reshape(E * H, C)[order], ((0, pad), (0, 0)))
    given = {
        "x_dram": a(x).reshape(T, C), "adj_dram": a(adj), "gnn_w1T_dram": a(L0_gnn_W1).T,
        "gnn_w2T_dram": a(L0_gnn_W2).T, "gnn_w3_dram": a(L0_gnn_W3), "router_dram": router,
        "w1T_dram": w1T, "w3T_dram": w3T, "w2_dram": w2,
    }
    given = {k: np.ascontiguousarray(v) for k, v in given.items()}

    nc = bacc.Bacc("TRN2", target_bir_lowering=False, num_devices=1)
    args = [nc.dram_tensor(k, v.shape, mybir.dt.from_np(v.dtype), kind="ExternalInput").ap()
            for k, v in given.items()]
    args.append(nc.dram_tensor("outT_dram", (C, T), mybir.dt.float32, kind="ExternalOutput").ap())
    bass_gnn_moe_kernel(nc, *args)
    got = run_bass_kernel_spmd(nc, [given], core_ids=[0]).results[0]["outT_dram"]
    return np.ascontiguousarray(got.T).reshape(BATCH, N, C)
```

```python
from contextlib import ExitStack

import concourse.bass as bass
from concourse import mybir


BATCH, N, C = 128, 64, 128
E, H = 8, 341
P = 128
T = BATCH * N
BT = 512
NB = T // BT
TI = BT // P
FULL = H // P
REST = H - FULL * P
PURE = E * FULL
ROWS = P // TI
MIXED = -(-E * REST // P)
CH = PURE + MIXED
LAG = 4
ALPHA, NEG, EPS, TOP_EPS = 0.2, 1e12, 1e-5, 1e-9
TINY = 2.0 ** -126

LAST = CH - 1
REMAIN = E * H - LAST * P
HALF = P // 2
assert REMAIN <= min(HALF, REST)

SEGMENTS = []
for _k in range(MIXED - 1):
    _p = 0
    while _p < P:
        _e = min((_k * P + _p) // REST, E - 1)
        _end = P if _e == E - 1 else min(P, (_e + 1) * REST - _k * P)
        SEGMENTS.append((_k, _p, _end, _e))
        _p = _end
RESIDUAL_AT = 9
SOON = 2
LATE_DMAS = 1 + len(SEGMENTS)

IDLE = range(29, 34)
HEAD = 15


def bass_gnn_moe_kernel(nc, x, adj, gnn_w1T, gnn_w2T, gnn_w3, routerT, w1T, w3T, w2, outT):
    fp32, fp32r, i32 = mybir.dt.float32, mybir.dt.float32r, mybir.dt.int32
    ALU, ACT, X = mybir.AluOpType, mybir.ActivationFunctionType, mybir.AxisListType.X
    PE, DVE, SCA, POOL, SP = nc.tensor, nc.vector, nc.scalar, nc.gpsimd, nc.sync

    x_blocks = x.rearrange("(b t p) c -> p b t c", t=TI, p=P)
    gate_rows = [nc.dram_tensor(f"gate_rows{i}", (E, BT), fp32).ap() for i in range(2)]

    with ExitStack() as ctx:
        def sb(name, shape, dt=fp32):
            return ctx.enter_context(nc.sbuf_tensor(name, shape, dt))

        def pair(name, shape, dt=fp32, n=2):
            return [sb(f"{name}{i}", shape, dt) for i in range(n)]

        def bank(name):
            return ctx.enter_context(nc.psum_tensor(name, [P, BT], fp32))

        def sem(name):
            return ctx.enter_context(nc.semaphore(name))

        ident = sb("ident", [P, P])
        adj_sb = sb("adj_sb", [P, N], i32)
        mask = sb("mask", [P, TI, N])
        no_edge = sb("no_edge", [P, TI, N])
        tie = sb("tie", [P, TI, E, E])
        minus_half, eps = sb("minus_half", [P, TI]), sb("eps", [P, TI])
        g1T, g2T, g3 = sb("g1T", [P, C]), sb("g2T", [P, C]), sb("g3", [P, C])
        scores_w = sb("scores_w", [P, C])
        rw = sb("rw", [P, P])
        rw_hi, rw_lo = sb("rw_hi", [P, P], fp32r), sb("rw_lo", [P, P], fp32r)
        w1_hi, w1_lo = sb("w1_hi", [P, CH, P], fp32r), sb("w1_lo", [P, CH, P], fp32r)
        w3_hi, w3_lo = sb("w3_hi", [P, LAST, P], fp32r), sb("w3_lo", [P, LAST, P], fp32r)
        w2_hi, w2_lo = sb("w2_hi", [P, CH, P], fp32r), sb("w2_lo", [P, CH, P], fp32r)
        gate = pair("gate", [P, E + MIXED, BT])
        w1_in = gate[1][:, 0:6, :].rearrange("p a b -> p (a b)")[:, 0:CH * P].rearrange("p (c k) -> p c k", k=P)
        w3_in = gate[1][:, 6:12, :].rearrange("p a b -> p (a b)")[:, 0:LAST * P].rearrange("p (c k) -> p c k", k=P)
        w2_in = gate[0][:, E:E + 6, :].rearrange("p a b -> p (a b)")[:, 0:CH * P].rearrange("p (c k) -> p c k", k=P)

        x_in = pair("x_in", [P, TI, C])
        stats = sb("stats", [P, TI, 6])
        apart, squares = sb("apart", [P, TI]), sb("squares", [P, TI])
        mean, var_eps, rstd = sb("mean", [P, TI]), sb("var_eps", [P, TI]), sb("rstd", [P, TI])
        xn = sb("xn", [P, TI, C])
        xnT = sb("xnT", [P, BT])
        qT = sb("qT", [P, BT])
        v = sb("v", [P, TI, C])
        small_e = sb("small_e", [P, TI, N])
        scores = sb("scores", [P, TI, N])
        row_max = sb("row_max", [P, TI])
        probs = sb("probs", [P, TI, P])
        row_sum = sb("row_sum", [P, TI])
        row_scale = sb("row_scale", [P, TI])
        probsT = sb("probsT", [P, TI, P])
        att = sb("att", [P, TI, C])
        x2 = pair("x2", [P, TI, C])
        mean2, var_eps2, rstd2 = sb("mean2", [P, TI]), sb("var_eps2", [P, TI]), sb("rstd2", [P, TI])
        xn2 = sb("xn2", [P, TI, C])
        xT_hi, xT_lo = pair("xT_hi", [P, BT], fp32r), pair("xT_lo", [P, BT], fp32r)
        logitsT = sb("logitsT", [P, P])
        logits = sb("logits", [P, TI, E])
        top = sb("top", [P, TI])
        shifted = sb("shifted", [P, TI, E])
        expo = sb("expo", [P, TI, E])
        total = sb("total", [P, TI])
        prob = sb("prob", [P, TI, E])
        above = sb("above", [P, TI, E, E])
        rank = sb("rank", [P, TI, E])
        gates = sb("gates", [P, TI, E])
        gatesT = sb("gatesT", [TI * E, P])
        act = pair("act", [P, BT])
        gated = pair("gated", [P, BT])
        hid = pair("hid", [P, BT], n=4)
        hid_hi, hid_lo = pair("hid_hi", [P, BT], fp32r, 4), pair("hid_lo", [P, BT], fp32r, 4)
        y_out = sb("y_out", [P, BT])
        residual = sb("residual", [P, BT])

        h1_ps, h3_ps = [bank("h1_ps0"), bank("h1_ps1")], [bank("h3_ps0"), bank("h3_ps1")]
        y_ps = bank("y_ps")
        A, B, D = bank("att_ps0"), bank("att_ps1"), bank("router_ps")

        gnn_in, adj_in, x_arrived = sem("gnn_in"), sem("adj_in"), sem("x_arrived")
        w1_arrived, w3_arrived, w2_arrived = sem("w1_arrived"), sem("w3_arrived"), sem("w2_arrived")
        pool_step, ident_set, consts_set, masks_set = (sem(n) for n in ("pool_step", "ident_set", "consts_set", "masks_set"))
        wprod_ps, wprod_set, edges_set = sem("wprod_ps"), sem("wprod_set"), sem("edges_set")
        hi_split, lo_split_dve, lo_split_pool = sem("hi_split"), sem("lo_split_dve"), sem("lo_split_pool")
        att_step = sem("att_step")
        moments_set, rstd_set, xn_set, xT_ps, xT_set = (sem(n) for n in ("moments_set", "rstd_set", "xn_set", "xT_ps", "xT_set"))
        q_ps, q_set, v_ps, v_set, e_ps = (sem(n) for n in ("q_ps", "q_set", "v_ps", "v_set", "e_ps"))
        small_set, leaky_set, kept_set, masked_set, shifted_set = (sem(n) for n in ("small_set", "leaky_set", "kept_set", "masked_set", "shifted_set"))
        probs_set, scale_set, pT_ps, pT_set, pv_ps = (sem(n) for n in ("probs_set", "scale_set", "pT_ps", "pT_set", "pv_ps"))
        att_set, x2_set = sem("att_set"), sem("x2_set")
        router_step = sem("router_step")
        moments2_set, rstd2_set, xn2_set, x2T_ps, xhi_set = (sem(n) for n in ("moments2_set", "rstd2_set", "xn2_set", "x2T_ps", "xhi_set"))
        xlo_set, lgT_ps, lgT_set, lg_ps, lg_shifted = (sem(n) for n in ("xlo_set", "lgT_ps", "lgT_set", "lg_ps", "lg_shifted"))
        lg_exp, gates_set, gT_ps, gT_set = (sem(n) for n in ("lg_exp", "gates_set", "gT_ps", "gT_set"))
        rows_written, gate_soon, gate_late = sem("rows_written"), sem("gate_soon"), sem("gate_late")
        h1_done, h3_done, act_set, gated_set = (sem(n) for n in ("h1_done", "h3_done", "act_set", "gated_set"))
        hid_set, hhi_set, hlo_set, w2_done = (sem(n) for n in ("hid_set", "hhi_set", "hlo_set", "w2_done"))
        residual_ps, residual_set, y_read = sem("residual_ps"), sem("residual_set"), sem("y_read")
        y_set, out_stored = sem("y_set"), sem("out_stored")

        graphs = [slice(0, N), slice(N, P)]

        def own_scores(at):
            return B[at, :].rearrange("p (t m) -> p t m", t=TI)[:, :, at]

        block = ctx.enter_context(nc.Block())

        def wait(eng, s, count):
            if not isinstance(count, int) or count > 0:
                eng.wait_ge(s, count)

        def used(c):
            return slice(0, HALF if c == LAST else P)

        def over_blocks(eng, start, prepare, multiply, finish=None):
            def turn(b, par, next_block=True, block_after=True):
                for c in range(CH):
                    multiply(b, par, c)
                    if next_block:
                        prepare(b + 1, 1 - par, CH + c)
                    if block_after:
                        prepare(b + 2, par, c)
                    if finish:
                        finish(b, par, c)

            if start:
                start()
            steps = [k for k in range(2 * CH) if k not in IDLE]
            for i in range(HEAD + CH):
                if i < len(steps):
                    prepare(0, 0, steps[i])
                if i >= HEAD:
                    prepare(1, 1, i - HEAD)
            turn(0, 0)
            with eng.Fori(0, (NB - 4) // 2) as i:
                turn(i * 2 + 1, 1)
                turn(i * 2 + 2, 0)
            turn(NB - 3, 1)
            turn(NB - 2, 0, block_after=False)
            turn(NB - 1, 1, next_block=False, block_after=False)

        @block.sync
        def _(sp):
            def load_x(n, par):
                wait(sp, moments_set, n)
                if isinstance(n, int) and n == 2:
                    sp.wait_ge(x2_set, 1)
                sp.dma_start(x_in[par][:], x_blocks[:, n] if isinstance(n, int) else
                             x_blocks[:, bass.ds(n, 1)].rearrange("p b t c -> p (b t) c")).then_inc(x_arrived, 16)

            def load_gates(n, par):
                sp.wait_ge(gT_set, n + 1)
                sp.dma_start(gate_rows[par].rearrange("e (t p) -> t e p", t=TI), gatesT[:]).then_inc(rows_written, 16)
                sp.wait_ge(rows_written, n * 16 + 16)
                if isinstance(n, int) and n == 0:
                    sp.wait_ge(lo_split_dve, 3)
                    sp.wait_ge(lo_split_pool, 1)
                for e0, e1, signal in ((0, SOON, gate_soon), (SOON, E, gate_late)):
                    sp.dma_start(gate[par][:, e0:e1, :].rearrange("p e t -> p (e t)"),
                                 gate_rows[par][e0:e1].rearrange("e t -> (e t)").partition_broadcast(P)).then_inc(signal, 16)
                for k, p0, p1, e in SEGMENTS:
                    sp.dma_start(gate[par][p0:p1, E + k, :],
                                 gate_rows[par][e].partition_broadcast(p1 - p0)).then_inc(gate_late, 16)

            def store_out(n):
                sp.wait_ge(y_set, n + 1)
                sp.dma_start(outT[:, bass.ds(n * BT, BT)], y_out[:]).then_inc(out_stored, 16)

            def start():
                load_x(0, 0)
                sp.dma_start(g1T[:], gnn_w1T).then_inc(gnn_in, 16)
                sp.dma_start(g2T[:], gnn_w2T).then_inc(gnn_in, 16)
                sp.dma_start(g3[:], gnn_w3).then_inc(gnn_in, 16)
                sp.dma_start(rw[:], routerT).then_inc(gnn_in, 16)
                sp.dma_start(adj_sb[0:N, :], adj).then_inc(adj_in, 16)
                sp.dma_start(adj_sb[N:P, :], adj).then_inc(adj_in, 16)
                sp.dma_start(w1_in, w1T.rearrange("c (k h) -> c k h", h=P)).then_inc(w1_arrived, 16)
                sp.dma_start(w3_in, w3T.rearrange("c (k h) -> c k h", h=P)).then_inc(w3_arrived, 16)
                sp.dma_start(w2_in, w2.rearrange("(k h) c -> h k c", h=P)).then_inc(w2_arrived, 16)
                load_x(1, 1)
                load_x(2, 0)
                load_gates(0, 0)

            def turn(b, par, load=True, gates=True):
                if load:
                    load_x(b + 3, 1 - par)
                if not isinstance(b, int) or b > 0:
                    store_out(b - 1)
                if gates:
                    load_gates(b + 1, 1 - par)

            start()
            turn(0, 0)
            with sp.Fori(0, (NB - 4) // 2) as i:
                turn(i * 2 + 1, 1)
                turn(i * 2 + 2, 0)
            turn(NB - 3, 1, load=False)
            turn(NB - 2, 0, load=False)
            turn(NB - 1, 1, load=False, gates=False)
            store_out(NB - 1)
            sp.wait_ge(out_stored, NB * 16)

        @block.tensor
        def _(pe):
            def split_product(out, hi_w, lo_w, hi_x, lo_x, start=True, stop=True):
                PE.matmul(out, hi_w, hi_x, start=start, stop=False, skip_group_check=True)
                PE.matmul(out, hi_w, lo_x, start=False, stop=False, skip_group_check=True)
                return PE.matmul(out, lo_w, hi_x, start=False, stop=stop, skip_group_check=True)

            def prepare(n, par, k):
                if k == 5:
                    pe.wait_ge(xn_set, n + 1)
                    wait(pe, pT_set, n)
                    for t in range(TI):
                        last = PE.transpose(A[:, t * P:(t + 1) * P], xn[:, t, :], ident[:])
                    last.then_inc(xT_ps, 1)
                if k == 7:
                    pe.wait_ge(xT_set, n + 1)
                    wait(pe, att_set, n)
                    PE.matmul(B[:], scores_w[:], xnT[:], start=True, stop=True).then_inc(q_ps, 1)
                if k == 8:
                    for t in range(TI):
                        last = PE.matmul(A[:, t * P:(t + 1) * P], xnT[:, t * P:(t + 1) * P], g3[:],
                                         start=True, stop=True, skip_group_check=True)
                    last.then_inc(v_ps, 1)
                if k == 9:
                    pe.wait_ge(q_set, n + 1)
                    for t in range(TI):
                        at = slice(t * P, (t + 1) * P)
                        last = PE.matmul(B[:, at], qT[:, at], xnT[:, at], start=True, stop=True,
                                         skip_group_check=True)
                    last.then_inc(e_ps, 1)
                if k == 14:
                    pe.wait_ge(probs_set, n + 1)
                    pe.wait_ge(v_set, n + 1)
                    for t in range(TI):
                        last = PE.transpose(A[:, t * P:(t + 1) * P], probs[:, t, :], ident[:])
                    last.then_inc(pT_ps, 1)
                if k == 16:
                    pe.wait_ge(pT_set, n + 1)
                    for t in range(TI):
                        last = PE.matmul(B[:, t * P:(t + 1) * P], probsT[:, t, :], v[:, t, :],
                                         start=True, stop=True, skip_group_check=True)
                    last.then_inc(pv_ps, 1)
                if k == 23:
                    pe.wait_ge(xn2_set, n + 1)
                    wait(pe, gT_set, n)
                    for t in range(TI):
                        last = PE.transpose(D[:, t * P:(t + 1) * P], xn2[:, t, :], ident[:])
                    last.then_inc(x2T_ps, 1)
                if k == 25:
                    pe.wait_ge(xlo_set, n + 1)
                    if isinstance(n, int) and n == 0:
                        pe.wait_ge(lo_split_dve, 1)
                    split_product(D[:], rw_hi[:], rw_lo[:], xT_hi[par][:], xT_lo[par][:]).then_inc(lgT_ps, 1)
                if k == 28:
                    pe.wait_ge(lgT_set, n + 1)
                    PE.transpose(D[:, 0:P], logitsT[:], ident[:]).then_inc(lg_ps, 1)
                if k == 39:
                    pe.wait_ge(gates_set, n + 1)
                    wait(pe, residual_set, n)
                    PE.transpose(D[0:TI * E, 0:P], gates[:].rearrange("p t e -> p (t e)"),
                                 ident[:]).then_inc(gT_ps, 1)

            def start():
                pe.wait_ge(gnn_in, 64)
                PE.matmul(B[:, 0:C], g1T[:], g2T[:], start=True, stop=True).then_inc(wprod_ps, 1)
                pe.wait_ge(ident_set, 1)
                pe.wait_ge(wprod_set, 1)

            def multiply(b, par, c):
                g, i = b * CH + c, par * CH + c
                if c == 0:
                    pe.wait_ge(xlo_set, b + 1)
                    if isinstance(b, int) and b == 0:
                        pe.wait_ge(lo_split_dve, 3)
                wait(pe, act_set, g - 1)
                if c == 1:
                    wait(pe, gated_set, g - 1)
                split_product(h1_ps[i % 2][:], w1_hi[:, c, :], w1_lo[:, c, :],
                              xT_hi[par][:], xT_lo[par][:]).then_inc(h1_done, 1)
                if c < LAST:
                    wait(pe, gated_set, g - 1)
                    split_product(h3_ps[i % 2][:], w3_hi[:, c, :], w3_lo[:, c, :],
                                  xT_hi[par][:], xT_lo[par][:]).then_inc(h3_done, 1)
                if c >= LAG:
                    pe.wait_ge(hlo_set, g - LAG + 1)
                    if c == LAG:
                        if isinstance(b, int) and b == 0:
                            pe.wait_ge(lo_split_pool, 1)
                        wait(pe, y_read, b)
                    split_product(y_ps[:], w2_hi[:, c - LAG, :], w2_lo[:, c - LAG, :],
                                  hid_hi[(i - LAG) % 4][:], hid_lo[(i - LAG) % 4][:],
                                  start=(c == LAG), stop=False).then_inc(w2_done, 1)
                elif not isinstance(b, int) or b > 0:
                    tail_product(b, par, c)
                if c == RESIDUAL_AT:
                    if isinstance(b, int) and b == NB - 1:
                        pe.wait_ge(gT_set, NB)
                    else:
                        pe.wait_ge(lg_shifted, b + 2)
                    for t in range(TI):
                        last = PE.transpose(D[:, t * P:(t + 1) * P], x2[par][:, t, :], ident[:])
                    last.then_inc(residual_ps, 1)

            def tail_product(b, par, c):
                g, i = b * CH + c - LAG, (par * CH + c - LAG) % 4
                k = CH - LAG + c
                pe.wait_ge(hlo_set, g + 1)
                rows = used(k)
                split_product(y_ps[:], w2_hi[rows, k, :], w2_lo[rows, k, :], hid_hi[i][rows, :], hid_lo[i][rows, :],
                              start=False, stop=(k == CH - 1)).then_inc(w2_done, 1)

            over_blocks(pe, start, prepare, multiply)
            for c in range(LAG):
                tail_product(NB, 0, c)

        @block.scalar
        def _(sc):
            def prepare(n, par, k):
                if k == 5:
                    sc.wait_ge(xT_ps, n + 1)
                    SCA.activation(xnT[:], A[:], ACT.Copy).then_inc(xT_set, 1)
                if k == 7:
                    sc.wait_ge(q_ps, n + 1)
                    SCA.activation(qT[:], B[:], ACT.Copy).then_inc(q_set, 1)
                if k == 9:
                    sc.wait_ge(e_ps, n + 1)
                    for at in graphs:
                        last = SCA.activation(small_e[at, :, :], own_scores(at), ACT.Copy, scale=ALPHA)
                    last.then_inc(small_set, 1)
                if k == 10:
                    sc.wait_ge(v_ps, n + 1)
                    SCA.activation(v[:].rearrange("p t c -> p (t c)"), A[:], ACT.Copy).then_inc(v_set, 1)
                if k == 12:
                    sc.wait_ge(shifted_set, n + 1)
                    for at in graphs:
                        last = SCA.activation(probs[at, :, at], scores[at, :, :], ACT.Exp)
                    last.then_inc(probs_set, 1)
                if k == 14:
                    sc.wait_ge(pT_ps, n + 1)
                    SCA.activation(probsT[:].rearrange("p t m -> p (t m)"), A[:], ACT.Copy).then_inc(pT_set, 1)
                if k == 16:
                    sc.wait_ge(pv_ps, n + 1)
                    sc.wait_ge(scale_set, n + 1)
                    for t in range(TI):
                        last = SCA.activation(att[:, t, :], B[:, t * P:(t + 1) * P], ACT.Relu,
                                              scale=row_scale[:, t:t + 1])
                    last.then_inc(att_set, 1)
                if k == 23:
                    sc.wait_ge(x2T_ps, n + 1)
                    wait(sc, h1_done, (n - 1) * CH)
                    SCA.activation(xT_hi[par][:], D[:], ACT.Copy).then_inc(xhi_set, 1)
                if k == 26:
                    sc.wait_ge(lgT_ps, n + 1)
                    for t in range(TI):
                        last = SCA.activation(logitsT[t * ROWS:t * ROWS + E, :], D[0:E, t * P:(t + 1) * P], ACT.Copy)
                    last.then_inc(lgT_set, 1)
                if k == 34:
                    sc.wait_ge(lg_shifted, n + 1)
                    SCA.activation(expo[:].rearrange("p t e -> p (t e)"),
                                   shifted[:].rearrange("p t e -> p (t e)"), ACT.Exp).then_inc(lg_exp, 1)
                if k == 40:
                    sc.wait_ge(gT_ps, n + 1)
                    wait(sc, rows_written, n * 16)
                    SCA.activation(gatesT[:], D[0:TI * E, 0:P], ACT.Copy).then_inc(gT_set, 1)
                if isinstance(n, int) and n == 0 and k in WEIGHTS_AT:
                    w_in, hi, arrived = WEIGHTS_AT[k]
                    sc.wait_ge(arrived, 16)
                    SCA.activation(hi[:], w_in, ACT.Copy).then_inc(hi_split, 1)

            EXPONENTIALS_AT = 12

            WEIGHTS_AT = {7: (w1_in, w1_hi, w1_arrived), 14: (w3_in, w3_hi, w3_arrived),
                          16: (w2_in, w2_hi, w2_arrived)}

            def coarse(g, i):
                sc.wait_ge(hid_set, g + 1)
                wait(sc, w2_done, g - 3)
                rows = used(i % CH)
                SCA.activation(hid_hi[i % 4][rows, :], hid[i % 4][rows, :], ACT.Copy).then_inc(hhi_set, 1)

            def start():
                sc.wait_ge(wprod_ps, 1)
                SCA.activation(scores_w[:], B[:, 0:C], ACT.Copy).then_inc(wprod_set, 1)
                SCA.activation(rw_hi[:], rw[:], ACT.Copy).then_inc(hi_split, 1)

            def multiply(b, par, c):
                g, i = b * CH + c, par * CH + c
                if c == RESIDUAL_AT + 1:
                    sc.wait_ge(residual_ps, b + 1)
                    wait(sc, y_set, b)
                    SCA.activation(residual[:], D[:], ACT.Copy).then_inc(residual_set, 1)
                sc.wait_ge(h1_done, g + 1)
                wait(sc, hid_set, g - 1)
                rows = used(c)
                SCA.activation(act[i % 2][rows, :], h1_ps[i % 2][rows, :], ACT.Silu).then_inc(act_set, 1)
                if c == LAG - 1 and (not isinstance(b, int) or b > 0):
                    result(b - 1)
                if c != EXPONENTIALS_AT and (not isinstance(g, int) or g > 0):
                    coarse(g - 1, i - 1)

            def finish(b, par, c):
                if c == EXPONENTIALS_AT:
                    coarse(b * CH + c - 1, par * CH + c - 1)

            def result(n):
                sc.wait_ge(w2_done, n * CH + CH)
                wait(sc, out_stored, n * 16)
                SCA.activation(y_out[:], y_ps[:], ACT.Copy).then_inc(y_read, 1)

            over_blocks(sc, start, prepare, multiply, finish)
            coarse(NB * CH - 1, 2 * CH - 1)
            result(NB - 1)

        @block.vector
        def _(dve):
            ATT_STEPS, ROUTER_STEPS = 6, 16

            def att(instruction, n, j):
                instruction.then_inc(att_step, 1)
                dve.wait_ge(att_step, n * ATT_STEPS + j)

            def router(instruction, n, j):
                instruction.then_inc(router_step, 1)
                dve.wait_ge(router_step, n * ROUTER_STEPS + j)

            def even_odd(source):
                for t in range(TI):
                    last = DVE.bn_stats(stats[:, t, :], source[:, t, :])
                return last

            def moments(mean, var_eps, step, n):
                DVE.tensor_tensor(mean[:], stats[:, :, 1], stats[:, :, 4], ALU.add)
                DVE.tensor_tensor(apart[:], stats[:, :, 1], stats[:, :, 4], ALU.subtract)
                step(DVE.tensor_tensor(squares[:], stats[:, :, 2], stats[:, :, 5], ALU.add), n, 2)
                DVE.tensor_scalar(mean[:], mean[:], 0.5, None, ALU.mult)
                step(DVE.tensor_tensor(apart[:], apart[:], apart[:], ALU.mult), n, 3)
                step(DVE.scalar_tensor_tensor(squares[:], apart[:], C / 4, squares[:], ALU.mult, ALU.add), n, 4)
                return DVE.tensor_scalar(var_eps[:], squares[:], 1 / C, EPS, ALU.mult, ALU.add)

            def normalise(out, source, mean, rstd, tiles):
                for t in tiles:
                    last = DVE.tensor_scalar(out[:, t, :], source[:, t, :], mean[:, t:t + 1],
                                             rstd[:, t:t + 1], ALU.subtract, ALU.mult)
                return last

            def per_token(a, m):
                return a[:].unsqueeze(2).broadcast_to([P, TI, m])

            def prepare(n, par, k):
                if k == 1:
                    dve.wait_ge(x_arrived, n * 16 + 16)
                    even_odd(x_in[par]).then_inc(att_step, 1)
                if k == 2:
                    dve.wait_ge(att_step, n * ATT_STEPS + 1)
                    moments(mean, var_eps, att, n).then_inc(moments_set, 1)
                if k == 3:
                    dve.wait_ge(rstd_set, n + 1)
                    wait(dve, xT_ps, n)
                    normalise(xn, x_in[par], mean, rstd, (0, 1))
                if k == 4:
                    normalise(xn, x_in[par], mean, rstd, (2, 3)).then_inc(xn_set, 1)
                    if isinstance(n, int) and n == 0:
                        constants()
                if k == 9:
                    dve.wait_ge(small_set, n + 1)
                    for at in graphs:
                        last = DVE.tensor_tensor(scores[at, :, :], own_scores(at), small_e[at, :, :], ALU.max)
                    last.then_inc(leaky_set, 1)
                if k == 11:
                    dve.wait_ge(masked_set, n + 1)
                    att(DVE.reduce_max(row_max[:], scores[:], axis=X), n, 5)
                    DVE.tensor_tensor(scores[:], scores[:], per_token(row_max, N), ALU.subtract).then_inc(shifted_set, 1)
                if k == 13:
                    dve.wait_ge(probs_set, n + 1)
                    att(DVE.reduce_sum(row_sum[:], probs[:], axis=X), n, 6)
                    DVE.reciprocal(row_scale[:], row_sum[:]).then_inc(scale_set, 1)
                if k == 18:
                    dve.wait_ge(x2_set, n + 1)
                    even_odd(x2[par]).then_inc(router_step, 1)
                if k == 19:
                    dve.wait_ge(router_step, n * ROUTER_STEPS + 1)
                    moments(mean2, var_eps2, router, n).then_inc(moments2_set, 1)
                if k == 20:
                    dve.wait_ge(rstd2_set, n + 1)
                    wait(dve, x2T_ps, n)
                    normalise(xn2, x2[par], mean2, rstd2, (0, 1))
                if k == 21:
                    normalise(xn2, x2[par], mean2, rstd2, (2, 3)).then_inc(xn2_set, 1)
                if k == 23:
                    dve.wait_ge(xhi_set, n + 1)
                    DVE.tensor_tensor(xT_lo[par][:], D[:], xT_hi[par][:].bitcast(fp32),
                                      ALU.subtract).then_inc(xlo_set, 1)
                if k == 28:
                    dve.wait_ge(lg_ps, n + 1)
                    router(DVE.tensor_copy(logits[:], D[:, 0:P].rearrange("p (t e) -> p t e", t=TI)[:, :, 0:E]), n, 5)
                    router(DVE.reduce_max(top[:], logits[:], axis=X), n, 6)
                    DVE.tensor_tensor(shifted[:], logits[:], per_token(top, E), ALU.subtract).then_inc(lg_shifted, 1)
                if k == 35:
                    dve.wait_ge(lg_exp, n + 1)
                    router(DVE.reduce_sum(total[:], expo[:], axis=X), n, 7)
                    router(DVE.reciprocal(top[:], total[:]), n, 8)
                    router(DVE.tensor_tensor(prob[:], expo[:], per_token(top, E), ALU.mult), n, 9)
                this = prob[:].unsqueeze(3).broadcast_to([P, TI, E, E])
                other = prob[:].unsqueeze(2).broadcast_to([P, TI, E, E])
                if k == 36:
                    router(DVE.tensor_tensor(above[:], other, this, ALU.subtract), n, 10)
                    DVE.tensor_tensor(above[:], above[:], tie[:], ALU.is_gt).then_inc(router_step, 1)
                if k == 37:
                    dve.wait_ge(router_step, n * ROUTER_STEPS + 11)
                    router(DVE.reduce_sum(rank[:], above[:], axis=X), n, 12)
                    router(DVE.scalar_tensor_tensor(gates[:], rank[:], 1.5, prob[:], ALU.is_lt, ALU.mult), n, 13)
                if k == 38:
                    router(DVE.reduce_sum(total[:], gates[:], axis=X), n, 14)
                    router(DVE.tensor_scalar_add(total[:], total[:], TOP_EPS), n, 15)
                    router(DVE.reciprocal(top[:], total[:]), n, 16)
                    DVE.tensor_tensor(gates[:], gates[:], per_token(top, E), ALU.mult).then_inc(gates_set, 1)
                if isinstance(n, int) and n == 0 and k in (11, 15):
                    w_in, hi, lo, count = {11: (w1_in, w1_hi, w1_lo, 2), 15: (w3_in, w3_hi, w3_lo, 3)}[k]
                    dve.wait_ge(hi_split, count)
                    DVE.tensor_tensor(lo[:], w_in, hi[:].bitcast(fp32), ALU.subtract).then_inc(lo_split_dve, 1)

            def fine(g, i):
                dve.wait_ge(hhi_set, g + 1)
                rows = used(i % CH)
                DVE.tensor_tensor(hid_lo[i % 4][rows, :], hid[i % 4][rows, :], hid_hi[i % 4][rows, :].bitcast(fp32),
                                  ALU.subtract).then_inc(hlo_set, 1)

            def constants():
                dve.wait_ge(adj_in, 32)
                DVE.tensor_scalar(mask[:], adj_sb[:].unsqueeze(1).broadcast_to([P, TI, N]), 0.0, None,
                                  ALU.is_gt).then_inc(edges_set, 1)
                dve.wait_ge(edges_set, 1)
                DVE.tensor_scalar(no_edge[:], mask[:], -1.0, NEG, ALU.add, ALU.mult)
                DVE.memset(logitsT[:], 0.0)
                DVE.memset(probs[:], 0.0).then_inc(masks_set, 1)
                dve.wait_ge(hi_split, 1)
                DVE.tensor_tensor(rw_lo[:], rw[:], rw_hi[:].bitcast(fp32), ALU.subtract).then_inc(lo_split_dve, 1)
                dve.wait_ge(consts_set, 1)

            def multiply(b, par, c):
                g, i = b * CH + c, par * CH + c
                weight = c // FULL if c < PURE else E + c - PURE
                if c == 0:
                    dve.wait_ge(gate_soon, b * 16 + 16)
                if c == SOON * FULL:
                    dve.wait_ge(gate_late, (b + 1) * (16 * LATE_DMAS))
                if c < LAST:
                    dve.wait_ge(h3_done, b * LAST + c + 1)
                else:
                    dve.wait_ge(act_set, g + 1)
                wait(dve, hid_set, g - 1)
                if c < LAST:
                    DVE.tensor_tensor(gated[i % 2][:], h3_ps[i % 2][:], gate[par][:, weight, :],
                                      ALU.mult).then_inc(gated_set, 1)
                else:
                    DVE.tensor_tensor(gated[i % 2][0:HALF, :], h1_ps[i % 2][HALF:P, :], gate[par][HALF:P, E - 1, :],
                                      ALU.mult).then_inc(gated_set, 1)
                if not isinstance(g, int) or g > 1:
                    fine(g - 2, i - 2)

            over_blocks(dve, None, prepare, multiply)
            for k in (2, 1):
                fine(NB * CH - k, 2 * CH - k)

        @block.gpsimd
        def _(pool):
            def prepare(n, par, k):
                if k == 2:
                    pool.wait_ge(moments_set, n + 1)
                    POOL.tensor_tensor(rstd[:], var_eps[:], minus_half[:], ALU.pow).then_inc(rstd_set, 1)
                if k == 10:
                    if isinstance(n, int) and n == 0:
                        pool.wait_ge(masks_set, 1)
                    pool.wait_ge(leaky_set, n + 1)
                    POOL.tensor_tensor(scores[:], scores[:], mask[:], ALU.mult).then_inc(kept_set, 1)
                    pool.wait_ge(kept_set, n + 1)
                    POOL.tensor_tensor(scores[:], scores[:], no_edge[:], ALU.add).then_inc(masked_set, 1)
                if k == 17:
                    pool.wait_ge(att_set, n + 1)
                    wait(pool, residual_ps, n - 1)
                    POOL.tensor_tensor(x2[par][:], x_in[par][:], att[:], ALU.add).then_inc(x2_set, 1)
                if k == 19:
                    pool.wait_ge(moments2_set, n + 1)
                    POOL.tensor_tensor(rstd2[:], var_eps2[:], minus_half[:], ALU.pow).then_inc(rstd2_set, 1)
                if isinstance(n, int) and n == 0 and k == 19:
                    pool.wait_ge(hi_split, 4)
                    POOL.tensor_tensor(w2_lo[:], w2_in, w2_hi[:].bitcast(fp32), ALU.subtract).then_inc(lo_split_pool, 1)

            def start():
                POOL.memset(ident[:], 0.0).then_inc(pool_step, 1)
                pool.wait_ge(pool_step, 1)
                POOL.affine_select(out=ident[:], in_=ident[:], compare_op=ALU.not_equal, fill=1.0, base=0,
                                   pattern=[[-1, P]], channel_multiplier=1).then_inc(ident_set, 1)
                POOL.memset(tie[:], -TINY).then_inc(pool_step, 1)
                pool.wait_ge(pool_step, 2)
                POOL.affine_select(out=tie[:], in_=tie[:], compare_op=ALU.is_gt, fill=0.0, base=0,
                                   pattern=[[0, TI], [1, E], [-1, E]], channel_multiplier=0).then_inc(consts_set, 1)
                POOL.memset(minus_half[:], -0.5).then_inc(pool_step, 1)
                pool.wait_ge(pool_step, 3)

            def multiply(b, par, c):
                g, i = b * CH + c, par * CH + c
                pool.wait_ge(act_set, g + 1)
                pool.wait_ge(gated_set, g + 1)
                wait(pool, hlo_set, g - 3)
                rows = used(c)
                POOL.tensor_tensor(hid[i % 4][rows, :], act[i % 2][rows, :], gated[i % 2][rows, :],
                                   ALU.mult).then_inc(hid_set, 1)
                if c == LAG + 1 and (not isinstance(b, int) or b > 0):
                    add_residual(b - 1)

            def add_residual(n):
                pool.wait_ge(y_read, n + 1)
                pool.wait_ge(residual_set, n + 1)
                POOL.tensor_tensor(y_out[:], y_out[:], residual[:], ALU.add).then_inc(y_set, 1)

            over_blocks(pool, start, prepare, multiply)
            add_residual(NB - 1)


def hidden_order():
    whole = [e * H + k for e in range(E) for k in range(FULL * P)]
    rest = [e * H + FULL * P + k for e in range(E) for k in range(REST)]
    return whole + rest


def kernel(x, adj, L0_gnn_W1, L0_gnn_W2, L0_gnn_W3, L0_ffn_router_w, L0_ffn_w1, L0_ffn_w2, L0_ffn_w3):
    import numpy as np
    import concourse.bacc as bacc
    from concourse.bass_utils import run_bass_kernel_spmd

    def a(v):
        return np.asarray(v)

    order = hidden_order()
    pad = CH * P - len(order)
    router = np.pad(a(L0_ffn_router_w).T, ((0, 0), (0, P - E)))
    w1T, w3T = (a(w).reshape(E * H, C)[order].T for w in (L0_ffn_w1, L0_ffn_w3))
    w1T, w3T, last = (np.pad(w, ((0, 0), (0, HALF - REMAIN))) for w in (w1T, w3T[:, :LAST * P], w3T[:, LAST * P:]))
    w1T, w3T = np.concatenate([w1T, last], axis=1), w3T[:, :LAST * P]
    w2 = np.pad(a(L0_ffn_w2).transpose(0, 2, 1).reshape(E * H, C)[order], ((0, pad), (0, 0)))
    given = {
        "x_dram": a(x).reshape(T, C), "adj_dram": a(adj), "gnn_w1T_dram": a(L0_gnn_W1).T,
        "gnn_w2T_dram": a(L0_gnn_W2).T, "gnn_w3_dram": a(L0_gnn_W3), "router_dram": router,
        "w1T_dram": w1T, "w3T_dram": w3T, "w2_dram": w2,
    }
    given = {k: np.ascontiguousarray(v) for k, v in given.items()}

    nc = bacc.Bacc("TRN2", target_bir_lowering=False, num_devices=1)
    args = [nc.dram_tensor(k, v.shape, mybir.dt.from_np(v.dtype), kind="ExternalInput").ap()
            for k, v in given.items()]
    args.append(nc.dram_tensor("outT_dram", (C, T), mybir.dt.float32, kind="ExternalOutput").ap())
    bass_gnn_moe_kernel(nc, *args)
    got = run_bass_kernel_spmd(nc, [given], core_ids=[0]).results[0]["outT_dram"]
    return np.ascontiguousarray(got.T).reshape(BATCH, N, C)
```
